# Optimizing a Trainium2 kernel written in Bass

```python
import numpy as np
import jax
import jax.numpy as jnp

def _softmax(x, axis=-1):
    return jax.nn.softmax(x, axis=axis)

def _gelu(x):
    return jax.nn.gelu(x, approximate=True)

def _silu(x):
    return jax.nn.silu(x)

def _sigmoid(x):
    return jax.nn.sigmoid(x)

def _layernorm(x, axis=-1, eps=1e-05):
    m = jnp.mean(x, axis=axis, keepdims=True)
    v = jnp.var(x, axis=axis, keepdims=True)
    return (x - m) / jnp.sqrt(v + eps)

def _scatter_add(tgt, idx, src, axis=0):
    return tgt.at[idx].add(src)

def _segment_sum(src, seg, n):
    return jax.ops.segment_sum(src, seg, n)
kernel_name = 'mk_perceiver_d1_seqx_r4_9be328'

def setup_inputs(seed: int=0):
    np.random.seed(seed)
    _w = jnp.asarray

    def _rec_inputs():
        import jax
        import jax.numpy as jnp
        _rk = jax.random.key(seed)
        x = 7.22e-05 + 1 * jax.random.normal(jax.random.fold_in(_rk, 1), (16, 64, 256), jnp.float32)
        _lenS = 64 - jax.random.randint(jax.random.fold_in(_rk, 7), (16,), 0, max(1, 64 // 4) + 1, jnp.int32)
        _lenS2 = 1601 - jax.random.randint(jax.random.fold_in(_rk, 8), (16,), 0, max(1, 1601 // 4) + 1, jnp.int32)
        _ctx_1024P = jax.random.normal(jax.random.fold_in(_rk, 11), (16, 16, 256), jnp.float32)
        _ctx_1024c = jax.random.dirichlet(jax.random.fold_in(_rk, 511), 0.3 * jnp.ones((16,), jnp.float32), (16, 1601))
        _ctx_1024t = jnp.einsum('bsk,bkd->bsd', _ctx_1024c, _ctx_1024P)
        _ctx_1024t = _ctx_1024t * jax.lax.rsqrt(jnp.mean(jnp.square(_ctx_1024t)) + 1e-12) * 0.953939
        ctx_1024 = 4.13588e-05 + 0.999923 * (_ctx_1024t + 0.3 * jax.random.normal(jax.random.fold_in(_rk, 611), (16, 1601, 256), jnp.float32))
        return (x, ctx_1024)
    x, ctx_1024 = _rec_inputs()

    def _L0_xattn_setup():
        import jax, jax.numpy as jnp
        import numpy as np
        D_MODEL = 256
        H = 16
        D_K = D_MODEL // H
        key = jax.random.key(seed)
        ks = jax.random.split(key, 11)
        B, S = (4, 512)
        scale = 1.0 / np.sqrt(D_MODEL)
        return {'Q': jax.random.normal(ks[0], (B, S, D_MODEL), jnp.float32), 'K': jax.random.normal(ks[1], (B, S, D_MODEL), jnp.float32), 'V': jax.random.normal(ks[2], (B, S, D_MODEL), jnp.float32), 'Wq': jax.random.normal(ks[3], (D_MODEL, D_MODEL), jnp.float32) * scale, 'bq': jnp.zeros((D_MODEL,), jnp.float32), 'Wk': jax.random.normal(ks[4], (D_MODEL, D_MODEL), jnp.float32) * scale, 'bk': jnp.zeros((D_MODEL,), jnp.float32), 'Wv': jax.random.normal(ks[5], (D_MODEL, D_MODEL), jnp.float32) * scale, 'bv': jnp.zeros((D_MODEL,), jnp.float32), 'Wo': jax.random.normal(ks[6], (D_MODEL, D_MODEL), jnp.float32) * scale, 'bo': jnp.zeros((D_MODEL,), jnp.float32)}
    _L0_xattn_all = _L0_xattn_setup()
    _L0_xattn_in = {k: v for k, v in _L0_xattn_all.items() if k in ('Wq', 'bq', 'Wk', 'bk', 'Wv', 'bv', 'Wo', 'bo')}
    del _L0_xattn_all

    def _L0_attn_setup():
        import jax, jax.numpy as jnp
        import numpy as np
        import math
        DIM = 256
        N_HEADS = 16
        HEAD_DIM = DIM // N_HEADS

        def get_sin_cos(seq_len, dim):
            theta = 10000.0 ** (-jnp.arange(0, dim, 2, dtype=jnp.float32) / dim)
            position = jnp.arange(seq_len, dtype=jnp.float32)
            freqs = position[:, None] * theta[None, :]
            emb = jnp.concatenate([jnp.sin(freqs), jnp.cos(freqs)], axis=-1)
            sin = emb[None, None]
            cos = emb[None, None]
            return (sin, cos)

        def rotate_half(x):
            x1, x2 = (x[..., ::2], x[..., 1::2])
            return jnp.concatenate([-x2, x1], axis=-1)

        def apply_rope(q, k):
            sin, cos = get_sin_cos(q.shape[2], q.shape[-1])
            q = q * cos + rotate_half(q) * sin
            k = k * cos + rotate_half(k) * sin
            return (q, k)
        key = jax.random.key(seed)
        ks = jax.random.split(key, 3)
        B, L, D = (2, 512, DIM)
        x = jax.random.normal(ks[0], (B, L, D), dtype=jnp.float32)
        Wqkv = jax.random.normal(ks[1], (D, 3 * D), dtype=jnp.float32) * (1.0 / math.sqrt(D))
        bqkv = jnp.zeros((3 * D,), dtype=jnp.float32)
        Wout = jax.random.normal(ks[2], (D, D), dtype=jnp.float32) * (1.0 / math.sqrt(D))
        bout = jnp.zeros((D,), dtype=jnp.float32)
        return {'x': x, 'Wqkv': Wqkv, 'bqkv': bqkv, 'Wout': Wout, 'bout': bout}
    _L0_attn_all = _L0_attn_setup()
    _L0_attn_in = {k: v for k, v in _L0_attn_all.items() if k in ('Wqkv', 'bqkv', 'Wout', 'bout')}
    del _L0_attn_all

    def _L0_ffn_setup():
        import jax, jax.numpy as jnp
        import numpy as np
        H = 256
        E = 8
        B, S = (4, 512)
        key = jax.random.key(seed)
        k1, k2, k3, k4 = jax.random.split(key, 4)
        x = jax.random.normal(k1, (B, S, H), dtype=jnp.float32)
        wg = jax.random.normal(k2, (H, E), dtype=jnp.float32) * 0.02
        W = jax.random.normal(k3, (E, H, H), dtype=jnp.float32) * 0.02
        b = jax.random.normal(k4, (E, H), dtype=jnp.float32) * 0.02
        return {'x': x, 'wg': wg, 'W': W, 'b': b}
    _L0_ffn_all = _L0_ffn_setup()
    _L0_ffn_in = {k: v for k, v in _L0_ffn_all.items() if k in ('wg', 'W', 'b')}
    del _L0_ffn_all
    return {'x': x, 'ctx_1024': ctx_1024, 'L0_xattn_Wq': _L0_xattn_in['Wq'], 'L0_xattn_bq': _L0_xattn_in['bq'], 'L0_xattn_Wk': _L0_xattn_in['Wk'], 'L0_xattn_bk': _L0_xattn_in['bk'], 'L0_xattn_Wv': _L0_xattn_in['Wv'], 'L0_xattn_bv': _L0_xattn_in['bv'], 'L0_xattn_Wo': _L0_xattn_in['Wo'], 'L0_xattn_bo': _L0_xattn_in['bo'], 'L0_attn_Wqkv': _L0_attn_in['Wqkv'], 'L0_attn_bqkv': _L0_attn_in['bqkv'], 'L0_attn_Wout': _L0_attn_in['Wout'], 'L0_attn_bout': _L0_attn_in['bout'], 'L0_ffn_wg': _L0_ffn_in['wg'], 'L0_ffn_W': _L0_ffn_in['W'], 'L0_ffn_b': _L0_ffn_in['b']}

def reference(x, ctx_1024, L0_xattn_Wq, L0_xattn_bq, L0_xattn_Wk, L0_xattn_bk, L0_xattn_Wv, L0_xattn_bv, L0_xattn_Wo, L0_xattn_bo, L0_attn_Wqkv, L0_attn_bqkv, L0_attn_Wout, L0_attn_bout, L0_ffn_wg, L0_ffn_W, L0_ffn_b):
    import jax
    import jax.numpy as jnp

    def _L0_xattn_ref(Q, K, V, Wq, bq, Wk, bk, Wv, bv, Wo, bo):
        import jax, jax.numpy as jnp
        import numpy as np
        D_MODEL = 256
        H = 16
        D_K = D_MODEL // H
        B, S, _ = Q.shape

        def proj(x, W, b):
            return (x @ W.T + b).reshape(B, -1, H, D_K).transpose(0, 2, 1, 3)
        q = proj(Q, Wq, bq)
        k = proj(K, Wk, bk)
        v = proj(V, Wv, bv)
        scores = jnp.einsum('bhqd,bhkd->bhqk', q, k) / jnp.sqrt(jnp.float32(D_K))
        attn = jax.nn.softmax(scores, axis=-1)
        ctx = jnp.einsum('bhqk,bhkd->bhqd', attn, v)
        ctx = ctx.transpose(0, 2, 1, 3).reshape(B, S, H * D_K)
        return ctx @ Wo.T + bo

    def _L0_attn_ref(x, Wqkv, bqkv, Wout, bout):
        import jax, jax.numpy as jnp
        import numpy as np
        import math
        DIM = 256
        N_HEADS = 16
        HEAD_DIM = DIM // N_HEADS

        def get_sin_cos(seq_len, dim):
            theta = 10000.0 ** (-jnp.arange(0, dim, 2, dtype=jnp.float32) / dim)
            position = jnp.arange(seq_len, dtype=jnp.float32)
            freqs = position[:, None] * theta[None, :]
            emb = jnp.concatenate([jnp.sin(freqs), jnp.cos(freqs)], axis=-1)
            sin = emb[None, None]
            cos = emb[None, None]
            return (sin, cos)

        def rotate_half(x):
            x1, x2 = (x[..., ::2], x[..., 1::2])
            return jnp.concatenate([-x2, x1], axis=-1)

        def apply_rope(q, k):
            sin, cos = get_sin_cos(q.shape[2], q.shape[-1])
            q = q * cos + rotate_half(q) * sin
            k = k * cos + rotate_half(k) * sin
            return (q, k)
        B, L, D = x.shape
        H, Hd = (N_HEADS, HEAD_DIM)
        qkv = (x @ Wqkv + bqkv).reshape(B, L, 3, H, Hd)
        q, k, v = (qkv[:, :, 0], qkv[:, :, 1], qkv[:, :, 2])
        q = q.transpose(0, 2, 1, 3)
        k = k.transpose(0, 2, 1, 3)
        v = v.transpose(0, 2, 1, 3)
        q, k = apply_rope(q, k)
        scores = jnp.einsum('bhqd,bhkd->bhqk', q, k) / math.sqrt(Hd)
        probs = jax.nn.softmax(scores, axis=-1)
        out = jnp.einsum('bhqk,bhkd->bhqd', probs, v)
        out = out.transpose(0, 2, 1, 3).reshape(B, L, D)
        return out @ Wout + bout

    def _L0_ffn_ref(x, wg, W, b):
        import jax, jax.numpy as jnp
        import numpy as np
        H = 256
        E = 8
        B, S = (4, 512)
        Bb, Ss, Hh = x.shape
        Ee = wg.shape[1]
        T = Bb * Ss
        C = T // Ee
        xt = x.reshape(T, Hh)
        logits = xt @ wg
        probs = jax.nn.softmax(logits, axis=-1)
        idx = jnp.argmax(probs, axis=-1)
        mask = jax.nn.one_hot(idx, Ee, dtype=xt.dtype)
        locations = jnp.cumsum(mask, axis=0) - mask
        mask = mask * (locations < C).astype(xt.dtype)
        gate = jnp.sum(probs * mask, axis=-1)
        loc_s = jnp.sum(locations * mask, axis=-1).astype(jnp.int32)
        loc_oh = jax.nn.one_hot(loc_s, C, dtype=xt.dtype)
        dispatch = mask[:, :, None] * loc_oh[:, None, :]
        combine = gate[:, None, None] * dispatch
        exp_in = jnp.einsum('tec,th->ech', dispatch, xt)
        exp_out = jnp.einsum('ech,efh->ecf', exp_in, W) + b[:, None, :]
        out = jnp.einsum('tec,ecf->tf', combine, exp_out)
        return out.reshape(Bb, Ss, Hh)
    x = x + _L0_xattn_ref(_layernorm(x, axis=-1), ctx_1024, ctx_1024, L0_xattn_Wq, L0_xattn_bq, L0_xattn_Wk, L0_xattn_bk, L0_xattn_Wv, L0_xattn_bv, L0_xattn_Wo, L0_xattn_bo)
    x = x + _L0_attn_ref(_layernorm(x, axis=-1), L0_attn_Wqkv, L0_attn_bqkv, L0_attn_Wout, L0_attn_bout)
    x = x + _L0_ffn_ref(_layernorm(x, axis=-1), L0_ffn_wg, L0_ffn_W, L0_ffn_b)
    return x

_drawn_inputs = setup_inputs


def setup_inputs(seed=0):
    import zlib

    import numpy as np

    out = dict(_drawn_inputs(seed))
    spreads = {'L0_xattn_bq': (0.0, 0.332),
     'L0_xattn_bk': (0.0, 0.8),
     'L0_xattn_bv': (0.0, 0.1),
     'L0_xattn_bo': (0.0, 0.1),
     'L0_attn_bqkv': (0.0, 0.1),
     'L0_attn_bout': (0.0, 0.1)}
    factors = {'L0_ffn_b': 8.0}
    for name, (base, spread) in spreads.items():
        noise = np.random.default_rng([zlib.crc32(name.encode()), seed]).standard_normal(out[name].shape)
        drawn = base * np.exp(spread * noise) if base else spread * noise
        out[name] = jnp.asarray(drawn.astype(out[name].dtype))
    for name, factor in factors.items():
        out[name] = (out[name] * factor).astype(out[name].dtype)
    return out
```

```python
import numpy as np
import concourse.bass as bass
from concourse import mybir
from contextlib import ExitStack

P = 128
D = 256
KT = D // P
HEADS = 16
DH = D // HEADS
B = 16
SQ = 64
SK = 1601
NCH = -(-SK // P)
SKP = SK + SK % 2
LAST = SK - (NCH - 1) * P
HP = HEADS // 2
TILES = B * SQ // P
E = 8
CAP = B * SQ // E
EPS = 1e-5
VW = 66
OW = 65
NPAR = 4
NSB = 3

C_ID, C_TRI, C_MASK, C_J, C_DESC, C_ROPE = 0, 128, 256, 264, 266, 274
NCONST = C_ROPE + 2 * DH

NPIECE = -(-SK // 512)
KUNITS = KT * NPIECE
VUNITS = -(-NCH // 2)
MUNITS = HP * NPIECE
NF = KUNITS + VUNITS + MUNITS + 2
F_V, F_M, F_S = KUNITS, KUNITS + VUNITS, KUNITS + VUNITS + MUNITS
SLOTS = [list(range(2 * k, 2 * k + 2)) for k in range(4)]
_m = F_M
for _k in range(4, NCH):
    _take = 3 if _k < 8 else 4
    SLOTS.append(([F_V + _k - 4] if _k - 4 < VUNITS else []) + list(range(_m, _m + _take)))
    _m += _take
SLOTS[-1] += [F_S, F_S + 1]
GPS_CHUNKS = [7, 8, 9, 10, 11, 12]
DVE_CHUNKS = [k for k in range(NCH) if k not in GPS_CHUNKS]


def piece(n):
    return n * 512, min(512, SK - n * 512)


def keys_of(k):
    return k * P, (P if k < NCH - 1 else LAST)


ONES2 = float(np.array([0x3F803F80], np.uint32).view(np.float32)[0])


class Step:

    def __init__(self, i, u):
        self.i, self.u, self.par = i, u, u % 2
        self.front = i is not None or u < B
        self.attend = i is not None or 1 <= u <= B
        self.tail = i is not None or u >= 2

    def at(self, n, c):
        return n * self.u + c if self.i is None else self.i * (2 * n) + (n * self.u + c)

    def half(self, c):
        return self.u // 2 + c if self.i is None else self.i + (self.u // 2 + c)


def wait(eng, sem, step, n, c):
    if step.i is None and n * step.u + c <= 0:
        return
    assert n * step.u + c > 0
    eng.wait_ge(sem, step.at(n, c))


def run_steps(eng, emit, upto, last):
    emit(Step(None, 0))
    emit(Step(None, 1))
    with eng.Fori(0, (upto - 2) // 2) as i:
        emit(Step(i, 2))
        emit(Step(i, 3))
    for u in range(upto, last):
        emit(Step(None, u))


def last_use(k, slots_now, slots_before):
    for j in range(k - 1, -1, -1):
        if slots_now[j] == slots_now[k]:
            return j
    n = len(slots_before)
    for j in range(n - 1, -1, -1):
        if slots_before[j] == slots_now[k]:
            return j - n
    raise ValueError(k)


POS = {f: n for n, f in enumerate(f for slot in SLOTS for f in slot)}
F_BANK = [n % 2 for n in range(NF)]
V_READ = POS[F_M - 1] + 1
S_BANK = [h % NSB for h in range(2 * NCH)]
P_SLOT = [[(k + par) % NPAR for k in range(NCH)] for par in range(2)]
F_PREV = [last_use(f, F_BANK, F_BANK) for f in range(NF)]
S_PREV = [last_use(h, S_BANK, S_BANK) for h in range(2 * NCH)]
P_PREV = [[last_use(k, P_SLOT[par], P_SLOT[1 - par]) for k in range(NCH)] for par in range(2)]


def build(nc, x, ctxT, wqT, wkT, wvT, bqk, woT, wqkv, wout, brows, wg, weT, be, consts, out):
    f32, bf16 = mybir.dt.float32, mybir.dt.bfloat16
    ALU, ACT, AX = mybir.AluOpType, mybir.ActivationFunctionType, mybir.AxisListType
    ctx = ExitStack()
    with ctx:
        def sb(name, shape, dt=f32):
            return ctx.enter_context(nc.sbuf_tensor(name, shape, dt))

        def sem(name):
            return ctx.enter_context(nc.semaphore(name))

        cst = sb("cst", [P, NCONST])
        ident, tri = cst[:, C_ID:C_ID + P], cst[:, C_TRI:C_TRI + P]
        mask8, jmask = cst[:, C_MASK:C_MASK + 8], cst[:, C_J:C_J + 2]
        desc, rope = cst[:, C_DESC:C_DESC + E], cst[:, C_ROPE:C_ROPE + 2 * DH]
        ident_bf = sb("ident_bf", [P, P], bf16)
        ones_f = sb("ones_f", [P, P])
        half_neg = sb("half_neg", [P, TILES])
        x_all = sb("x_all", [P, TILES * D])
        att_all = sb("att_all", [P, TILES * D])
        cbuf = [sb(f"cbuf{p}", [P, KT, SK]) for p in range(2)]
        clow = [sb(f"clow{p}", [P, KT, SK], bf16) for p in range(2)]
        khigh = sb("khigh", [P, KT, SK], bf16)
        klow = sb("klow", [P, KT, SK], bf16)
        kstack = [sb(f"kstack{p}", [P, HP, SKP], bf16) for p in range(2)]
        vstack = [sb(f"vstack{p}", [P, NCH, HP, VW], bf16) for p in range(2)]
        qstack = [sb(f"qstack{p}", [P, HP, P], bf16) for p in range(2)]
        prob = [sb(f"prob{p}", [P, HP * P]) for p in range(NPAR)]
        plow = [sb(f"plow{p}", [P, HP * P], bf16) for p in range(NPAR)]
        maxes = sb("maxes", [P, HP, NPIECE])
        negmax = sb("negmax", [P, HP])
        mparts = sb("mparts", [P, HP, 2], bf16)
        osb2 = sb("osb", [P, 2, 4 * OW])
        osb = osb2[:, :, :].rearrange("p a (h c) -> p (a h) c", c=OW)
        osum = sb("osum", [P, HP, 2 * DH])
        orec = sb("orec", [P, HP])
        w_f = [att_all[:, n * KT * D:(n + 1) * KT * D].rearrange("p (k n) -> p k n", k=KT) for n in range(2)]
        w_hi = [sb(f"w_hi{n}", [P, KT, D], bf16) for n in range(2)]
        w_lo = [sb(f"w_lo{n}", [P, KT, D], bf16) for n in range(2)]
        bcol = sb("bcol", [P, 2, KT])
        bq4 = sb("bq4", [P, KT])

        wq_sb = prob[0][:, 0:KT * D].rearrange("p (k n) -> p k n", k=KT)
        h0 = prob[1][:, :].rearrange("p (t n) -> p t n", n=D)
        h0T = cbuf[1][:, 0, 0:0 + 1024]
        h0T2 = cbuf[1][:, 1, 0:0 + 1024]
        qT = [prob[2], prob[3]]
        qhi = [plow[0], plow[1]]
        qlo = [plow[2], plow[3]]
        qbd_hi = kstack[1][:, 0:4, :].rearrange("p a n -> p (a n)")[:, 0:B * 2 * P]\
            .rearrange("p (b t c) -> p b t c", b=B, t=KT)
        qbd_lo = kstack[1][:, 4:8, :].rearrange("p a n -> p (a n)")[:, 0:B * 2 * P]\
            .rearrange("p (b t c) -> p b t c", b=B, t=KT)
        q_dram = [nc.dram_tensor(f"q_parts{n}", [B, P, KT, P], bf16, kind="Internal").ap() for n in range(2)]
        st0 = sb("st0", [P, TILES, 6])
        mv0 = sb("mv0", [P, TILES, 2])
        ve0 = sb("ve0", [P, TILES])
        rs0 = sb("rs0", [P, TILES])

        wo_sb = sb("wo_sb", [P, KT, D])
        wqkv_sb = sb("wqkv_sb", [P, KT, 3 * D])
        wout_sb = sb("wout_sb", [P, KT, D])
        wg_sb = sb("wg_sb", [P, KT, E])
        be_sb = sb("be_sb", [E, D])
        brow = sb("brow", [P, 6, D])
        we_sb = [cbuf[k][:, :, :].rearrange("p k n -> p (k n)")[:, 0:E * D] for k in range(KT)]
        room = kstack[0][:, :, :].rearrange("p a n -> p (a n)").bitcast(f32)
        kbd = room[:, 0:2048].rearrange("p (g b n) -> p g b n", g=2, b=2)
        sc = room[:, 2048:3072].rearrange("p (g n) -> p g n", g=2)
        qk, rot = room[:, 3072:3584], room[:, 3584:4096]
        pT = room[:, 4096:5120].rearrange("p (h n) -> p h n", h=HP)
        h1, att2 = room[:, 5120:5376], room[:, 5376:5632]
        att_b, xb = room[:, 5632:5888], room[:, 5888:6144]
        room1 = kstack[1][:, :, :].rearrange("p a n -> p (a n)").bitcast(f32)
        x1, x2, x2b, h2, y = (room1[:, n * D:(n + 1) * D] for n in range(5))
        attT, h1T, att2T, h2T = (room1[:, (5 + n) * D:(6 + n) * D].rearrange("p (k n) -> p k n", k=KT) for n in range(4))
        qkT = room1[:, 9 * D:11 * D].rearrange("p (k n) -> p k n", k=4)
        vbd = [sb(f"vbd{b}", [P, HP, 2, DH]) for b in range(2)]
        smax, ssum, srec = sb("smax", [P, HEADS]), sb("ssum", [P, HEADS]), sb("srec", [P, HEADS])
        stats, mv, ve, rs = sb("stats", [P, 2, 6]), sb("mv", [P, 2, 2]), sb("ve", [P, 2]), sb("rs", [P, 2])
        lg, ex, eq, mask, keep, wgt, cum = (sb(n, [P, E]) for n in ("lg", "ex", "eq", "mask", "keep", "wgt", "cum"))
        one1 = sb("one1", [P, 6])
        wT = sb("wT", [E, P])

        ps_front = ctx.enter_context(nc.psum_tensor("ps_front", [P, 2, 512], f32))
        ps_score = ctx.enter_context(nc.psum_tensor("ps_score", [P, NSB, 512], f32))
        ps_out = ctx.enter_context(nc.psum_tensor("ps_out", [P, 2, 512], f32))
        ps_tile = ctx.enter_context(nc.psum_tensor("ps_tile", [P, 512], f32))

        ld_x, ld_c, ld_w, ld_wq, ld_b, ld_t, ld_e = (
            sem(n) for n in ("ld_x", "ld_c", "ld_w", "ld_wq", "ld_b", "ld_t", "ld_e"))
        ones_set, chain0, ve0_rdy, rs0_rdy = (sem(n) for n in ("ones_set", "chain0", "ve0_rdy", "rs0_rdy"))
        fills_set = sem("fills_set")
        h0_rdy, h0T_ps, h0T_rdy, q_ps, q_rdy, qbd_rdy, q_sent, w_rdy = (
            sem(n) for n in ("h0_rdy", "h0T_ps", "h0T_rdy", "q_ps", "q_rdy", "qbd_rdy", "q_sent", "w_rdy"))
        c_loaded = [sem("c_loaded0"), sem("c_loaded1")]
        q_loaded = sem("q_loaded")
        k_stacked = [sem("k_stacked0"), sem("k_stacked1")]
        clow_done = sem("clow_done")
        front_done, front_free, high_done = sem("front_done"), sem("front_free"), sem("high_done")
        max_done, shift_ready = sem("max_done"), sem("shift_ready")
        score_done, exp_done, pv_done = sem("score_done"), sem("exp_done"), sem("pv_done")
        plow_dve, plow_gps = sem("plow_dve"), sem("plow_gps")
        out_copied, out_summed, att_done = sem("out_copied"), sem("out_summed"), sem("att_done")

        ev = {n: sem("t_" + n) for n in (
            "att_b", "attT_ps", "attT", "o_ps", "xb", "x1", "st1", "ag1", "ve1", "rs1",
            "h1", "h1T_ps", "h1T", "qk_ps", "qk", "v_ps", "v", "rotA", "rotB", "rot",
            "rT_ps", "rT", "kbd", "s_ps0", "s_ps1", "smax0", "smax1", "sub0", "sub1", "sexp",
            "ssum", "srec", "pT_ps0", "pT_ps1", "pT0", "pT1", "pv_ps", "att2", "att2T_ps", "att2T",
            "w_ps", "x1b", "x2", "st2", "ag2", "ve2", "rs2", "h2", "h2T_ps", "h2T",
            "lg_ps", "lg", "lmax", "lneg", "eqd", "eqm", "mask", "ex", "gate", "loc_ps",
            "keep", "cum", "wgt", "wT_ps", "wT", "b_ps", "y0", "y", "out",
            "e_ps0", "e_ps1", "e_ps2", "e_ps3")}
        y_step = sem("t_y_step")

        block = ctx.enter_context(nc.Block())

        def c_high(par, k, n0, n):
            return cbuf[par][:, k, :].bitcast(bf16)[:, 2 * n0 + 1:2 * (n0 + n):2]

        def p_high(slot, c0, n):
            return prob[slot][:, :].bitcast(bf16)[:, 2 * c0 + 1:2 * (c0 + n):2]

        @block.sync
        def _(sp):
            sp.dma_start(x_all[:, :].rearrange("p (t d) -> p t d", t=TILES),
                         x.rearrange("(t p) d -> p t d", p=P)).then_inc(ld_x, 16)
            sp.dma_start(wq_sb, wqT.rearrange("(k p) n -> p k n", p=P)).then_inc(ld_wq, 16)
            sp.dma_start(cbuf[0][:, :, :], ctxT[0].rearrange("(k p) n -> p k n", p=P)).then_inc(c_loaded[0], 16)

            def steps(step):
                par = step.par
                now, nxt = step.at(1, 0), step.at(1, 2)
                wait(sp, score_done, step, 2 * NCH, -2 * NCH)
                sp.wait_ge(q_sent, 32)
                for g, n in enumerate((0, 0, 1)):
                    src = q_dram[n][bass.ds(now, 1)] if step.i is not None else q_dram[n][step.u:step.u + 1]
                    for r in range(4):
                        sp.dma_start(qstack[par][32 * g:32 * g + 32, :, :]
                                     .rearrange("p (t r) c -> p r t c", r=4)[:, r],
                                     src[0, 32 * r:32 * r + 32]).then_inc(q_loaded, 16)
                for t in range(KT):
                    wait(sp, front_free, step, NF, NPIECE * (t + 1))
                    for g, src in enumerate((khigh, klow, khigh)):
                        for r in range(4):
                            sp.dma_start(kstack[par][32 * g:32 * g + 32, 4 * t + r, 0:SK],
                                         src[32 * r:32 * r + 32, t, :]).then_inc(k_stacked[t], 16)
                if step.i is not None or step.u + 2 < B:
                    wait(sp, front_done, step, NF, V_READ)
                    src = ctxT[nxt] if step.i is None else ctxT[bass.ds(nxt, 1)][0]
                    sp.dma_start(cbuf[par][:, :, :], src.rearrange("(k p) n -> p k n", p=P))\
                        .then_inc(c_loaded[par], 16)

            sp.wait_ge(q_ps, 4)
            sp.dma_start(cbuf[1][:, :, :], ctxT[1].rearrange("(k p) n -> p k n", p=P)).then_inc(c_loaded[1], 16)
            sp.wait_ge(qbd_rdy, 4)
            sp.dma_start(q_dram[0].rearrange("b p t c -> p b t c"), qbd_hi).then_inc(q_sent, 16)
            sp.dma_start(q_dram[1].rearrange("b p t c -> p b t c"), qbd_lo).then_inc(q_sent, 16)
            sp.wait_ge(q_sent, 32)
            run_steps(sp, steps, B - 2, B)
            sp.wait_ge(front_done, NF * (B - 1) + V_READ)
            for k in range(KT):
                sp.dma_start(we_sb[k].rearrange("p (e n) -> p e n", e=E),
                             weT.rearrange("e (k p) n -> k p e n", p=P)[k]).then_inc(ev["out"] if k else ld_e, 16)
            with sp.Fori(0, TILES) as tile:
                row = sp.snap(tile * P)
                sp.wait_ge(ev["y"], tile + 1)
                sp.wait_ge(ld_x, 16)
                sp.dma_start(out[bass.ds(row, P), :], y[:, :]).then_inc(ev["out"], 16)
            sp.wait_ge(ev["out"], 16 * TILES + 16)
        @block.gpsimd
        def _(pool):
            nc.gpsimd.memset(ones_f[:, :], 1.0).then_inc(ones_set, 1)
            nc.gpsimd.memset(half_neg[:, :], -0.5).then_inc(ones_set, 1)
            pool.dma_start(cst[:, :], consts).then_inc(ld_c, 16)
            pool.dma_start(w_f[0][:, :, :], wkT.rearrange("(k p) n -> p k n", p=P)).then_inc(ld_w, 16)
            pool.dma_start(w_f[1][:, :, :], wvT.rearrange("(k p) n -> p k n", p=P)).then_inc(ld_w, 16)
            pool.dma_start(bcol[:, :, :], bqk).then_inc(ld_b, 16)
            pool.dma_start(wo_sb[:, :, :], woT.rearrange("(k p) n -> p k n", p=P)).then_inc(ld_t, 16)
            pool.dma_start(wqkv_sb[:, :, :], wqkv.rearrange("(k p) n -> p k n", p=P)).then_inc(ld_t, 16)
            pool.dma_start(wout_sb[:, :, :], wout.rearrange("(k p) n -> p k n", p=P)).then_inc(ld_t, 16)
            pool.dma_start(wg_sb[:, :, :], wg.rearrange("(k p) n -> p k n", p=P)).then_inc(ld_t, 16)
            pool.dma_start(be_sb[:, :], be).then_inc(ld_t, 16)
            pool.dma_start(brow[:, :, :].rearrange("p a n -> p (a n)"), brows.partition_broadcast(P)).then_inc(ld_t, 16)
            pool.wait_ge(ones_set, 2)
            pool.wait_ge(ve0_rdy, 1)
            nc.gpsimd.tensor_tensor(rs0[:, :], ve0[:, :], half_neg[:, :], ALU.pow).then_inc(rs0_rdy, 1)

            def low_context(step, par):
                for k in range(KT):
                    for a, n in ((0, 801), (801, 800)):
                        nc.gpsimd.tensor_tensor(clow[par][:, k, a:a + n], cbuf[par][:, k, a:a + n],
                                                c_high(par, k, a, n), ALU.subtract).then_inc(clow_done, 1)

            pool.wait_ge(c_loaded[0], 16)
            low_context(None, 0)

            def steps(step):
                par = step.par
                if step.i is not None or step.u + 1 < B:
                    pool.wait_ge(c_loaded[1 - par], ctx_value(step))
                    wait(pool, front_done, step, NF, -NF + V_READ)
                    low_context(step, 1 - par)
                if step.attend:
                    b = 1 - par
                    for k in GPS_CHUNKS:
                        _, n = keys_of(k)
                        slot = P_SLOT[b][k]
                        wait(pool, exp_done, step, 2 * NCH, 2 * k + 2 - 2 * NCH)
                        wait(pool, pv_done, step, NCH, P_PREV[b][k] + 1 - NCH)
                        nc.gpsimd.tensor_tensor(plow[slot][0:n, :], prob[slot][0:n, :], p_high(slot, 0, HP * P)[0:n],
                                                ALU.subtract).then_inc(plow_gps, 1)

            def ctx_value(step):
                if step.i is None:
                    return 16 * ((step.u + 1) // 2 + 1)
                return step.i * 16 + 16 * ((step.u + 1) // 2 + 1)

            run_steps(pool, steps, B - 2, B + 2)
            with pool.Fori(0, TILES) as tile:
                for n in range(2):
                    pool.wait_ge(ev[("ve1", "ve2")[n]], tile + 1)
                    nc.gpsimd.tensor_tensor(rs[:, n:n + 1], ve[:, n:n + 1], half_neg[:, 0:1], ALU.pow)\
                        .then_inc(ev[("rs1", "rs2")[n]], 1)

        @block.tensor
        def _(pe):
            pe.wait_ge(ld_c, 16)
            for t in range(TILES):
                pe.wait_ge(h0_rdy, t + 1)
                if t >= 2:
                    pe.wait_ge(h0T_rdy, t - 1)
                for k in range(KT):
                    mm = nc.tensor.transpose(ps_front[:, t % 2, k * P:(k + 1) * P],
                                             h0[:, t % 4, k * P:(k + 1) * P], ident)
                mm.then_inc(h0T_ps, 1)
            pe.wait_ge(ld_wq, 16)
            pe.wait_ge(h0T_rdy, TILES)
            for o in range(KT):
                for half in range(2):
                    for k, hT in enumerate((h0T, h0T2)):
                        mm = nc.tensor.matmul(ps_score[:, half, :] if o == 0 else ps_out[:, half, :],
                                              wq_sb[:, k, o * P:(o + 1) * P], hT[:, half * 512:half * 512 + 512],
                                              start=(k == 0), stop=(k == KT - 1))
                    mm.then_inc(q_ps, 1)
            pe.wait_ge(w_rdy, 4)

            def front_unit(step, f):
                par = step.par
                bank = ps_front[:, F_BANK[POS[f]], :]
                wait(pe, front_free, step, NF, F_PREV[POS[f]] + 1)
                if f < F_V:
                    t, n = divmod(f, NPIECE)
                    n0, nn = piece(n)
                    terms = [(w, c, k) for k in range(KT) for w, c in ((w_hi, 0), (w_hi, 1), (w_lo, 0))]
                    for j, (w, c, k) in enumerate(terms):
                        rhs = clow[par][:, k, n0:n0 + nn] if c else c_high(par, k, n0, nn)
                        mm = nc.tensor.matmul(bank[:, 0:nn], w[0][:, k, t * P:(t + 1) * P], rhs,
                                              start=(j == 0), stop=(j == len(terms) - 1))
                elif f < F_M:
                    for a, c in enumerate(range(2 * (f - F_V), min(2 * (f - F_V) + 2, NCH))):
                        n0, nn = keys_of(c)
                        terms = [(w, hi, k) for k in range(KT) for w, hi in ((w_hi, 1), (w_lo, 1), (w_hi, 0))]
                        for j, (w, hi, k) in enumerate(terms):
                            lhs = c_high(par, k, n0, nn) if hi else clow[par][:, k, n0:n0 + nn]
                            mm = nc.tensor.matmul(bank[0:nn, a * D:(a + 1) * D], lhs, w[1][:, k, :],
                                                  start=(j == 0), stop=(j == len(terms) - 1))
                elif f < F_S:
                    hp, n = divmod(f - F_M, NPIECE)
                    n0, nn = piece(n)
                    if hp % 4 == 0 and n == 0:
                        wait(pe, k_stacked[hp // 4], step, 192, 192)
                        wait(pe, q_loaded, step, 192, 192)
                    mm = nc.tensor.matmul(bank[:, 0:nn], qstack[par][0:96, hp, :], kstack[par][0:96, hp, n0:n0 + nn],
                                          start=True, stop=True)
                else:
                    wait(pe, shift_ready, step, 1, 1)
                    for j in range(4):
                        hp = 4 * (f - F_S) + j
                        mm = nc.tensor.matmul(bank[96:98, j * P:(j + 1) * P], mparts[:, hp, :], ident_bf[:, :],
                                              start=True, stop=True, tile_position=(0, 96))
                mm.then_inc(front_done, 1)

            def score_half(step, h):
                k, e = divmod(h, 2)
                n0, nn = keys_of(k)
                par = 1 - step.par
                wait(pe, exp_done, step, 2 * NCH, S_PREV[h] + 1 - 2 * NCH)
                for j in range(4):
                    hp = 4 * e + j
                    mm = nc.tensor.matmul(ps_score[0:nn, S_BANK[h], j * P:(j + 1) * P],
                                          kstack[par][0:98, hp, n0:n0 + nn], qstack[par][0:98, hp, :],
                                          start=True, stop=True)
                mm.then_inc(score_done, 1)

            def weigh(step, k, back):
                b = (step.par + back) % 2
                n0, nn = keys_of(k)
                slot = P_SLOT[b][k]
                if k in GPS_CHUNKS:
                    wait(pe, plow_gps, step, len(GPS_CHUNKS), GPS_CHUNKS.index(k) + 1 - back * len(GPS_CHUNKS))
                else:
                    wait(pe, plow_dve, step, len(DVE_CHUNKS), DVE_CHUNKS.index(k) + 1 - back * len(DVE_CHUNKS))
                if k == 0:
                    wait(pe, out_copied, step, 1, -back)
                for hp in range(HP):
                    o = ps_out[:, hp // 4, (hp % 4) * OW:(hp % 4 + 1) * OW]
                    for part in range(2):
                        lhs = plow[slot][0:nn, hp * P:(hp + 1) * P] if part else p_high(slot, hp * P, P)[0:nn]
                        mm = nc.tensor.matmul(o, lhs, vstack[b][0:nn, k, hp, 0:OW],
                                              start=(k == 0 and part == 0 and hp % 4 == 0),
                                              stop=(k == NCH - 1 and part == 1 and hp % 4 == 3),
                                              skip_group_check=True)
                mm.then_inc(pv_done, 1)

            def steps(step):
                for k in range(NCH):
                    if k >= 2 and step.attend:
                        weigh(step, k - 2, 1)
                    if k < 2 and step.tail:
                        weigh(step, NCH - 2 + k, 2)
                    if step.attend:
                        if k == 0:
                            if step.i is None and step.u == 1:
                                pe.wait_ge(fills_set, 6)
                            wait(pe, front_free, step, NF, 0)
                        score_half(step, 2 * k)
                        score_half(step, 2 * k + 1)
                    if step.front:
                        if k == 0:
                            pe.wait_ge(c_loaded[step.par], step.half(1) * 16)
                            wait(pe, clow_done, step, 4, 4)
                        for f in SLOTS[k]:
                            front_unit(step, f)

            run_steps(pe, steps, B, B + 2)

            def transposes(src, n, need, free, done, tile):
                pe.wait_ge(ev[need], tile + 1)
                if free is not None:
                    pe.wait_ge(ev[free[0]], tile + free[1])
                for j in range(n):
                    mm = nc.tensor.transpose(ps_tile[:, j * P:(j + 1) * P], src[:, j * P:(j + 1) * P], ident)
                mm.then_inc(ev[done], 1)

            def product(lhsT, rhs, n, need, free, done, tile):
                pe.wait_ge(ev[need], tile + 1)
                if free is not None:
                    pe.wait_ge(ev[free], tile + 1)
                for k in range(KT):
                    mm = nc.tensor.matmul(ps_tile[:, 0:n], lhsT[:, k, :], rhs(k), start=(k == 0), stop=(k == KT - 1))
                mm.then_inc(ev[done], 1)

            pe.wait_ge(ld_t, 16 * 6)
            pe.wait_ge(ld_e, 16)
            pe.wait_ge(ev["out"], 16)
            pe.wait_ge(ones_set, 2)
            with pe.Fori(0, TILES) as tile:
                transposes(att_b, 2, "att_b", None, "attT_ps", tile)
                product(attT, lambda k: wo_sb[:, k, :], D, "attT", None, "o_ps", tile)
                transposes(h1, 2, "h1", None, "h1T_ps", tile)
                product(h1T, lambda k: wqkv_sb[:, k, 0:2 * D], 2 * D, "h1T", None, "qk_ps", tile)
                product(h1T, lambda k: wqkv_sb[:, k, 2 * D:3 * D], D, "qk", None, "v_ps", tile)
                transposes(rot, 4, "rot", ("v", 1), "rT_ps", tile)
                for g in range(2):
                    pe.wait_ge(ev["kbd"], tile + 1)
                    if g == 1:
                        pe.wait_ge(ev["sub0"], tile + 1)
                    for b in range(2):
                        mm = nc.tensor.matmul(ps_tile[64 * b:64 * b + 64, :], qkT[:, g, 64 * b:64 * b + 64], kbd[:, g, b, :],
                                              start=True, stop=True)
                    mm.then_inc(ev[f"s_ps{g}"], 1)
                for g in range(2):
                    transposes(sc[:, g, :], 4, "sexp", ("sub1", 1) if g == 0 else ("pT0", 1), f"pT_ps{g}", tile)
                pe.wait_ge(ev["pT1"], tile + 1)
                for hp in range(HP):
                    for b in range(2):
                        mm = nc.tensor.matmul(ps_tile[64 * b:64 * b + 64, hp * 32:(hp + 1) * 32],
                                              pT[:, hp, 64 * b:64 * b + 64],
                                              vbd[b][:, hp, :, :].rearrange("p j d -> p (j d)"), start=True, stop=True)
                mm.then_inc(ev["pv_ps"], 1)
                transposes(att2, 2, "att2", None, "att2T_ps", tile)
                product(att2T, lambda k: wout_sb[:, k, :], D, "att2T", None, "w_ps", tile)
                transposes(h2, 2, "h2", None, "h2T_ps", tile)
                product(h2T, lambda k: wg_sb[:, k, :], E, "h2T", None, "lg_ps", tile)
                pe.wait_ge(ev["mask"], tile + 1)
                pe.wait_ge(ev["cum"], tile + 1)
                nc.tensor.matmul(ps_tile[:, 0:E], tri, mask[:, :], start=True, stop=False)
                nc.tensor.matmul(ps_tile[:, 0:E], ones_f[:, :], cum[:, :], start=False, stop=True).then_inc(ev["loc_ps"], 1)
                pe.wait_ge(ev["wgt"], tile + 1)
                nc.tensor.transpose(ps_tile[0:E, 0:P], wgt[:, :], ident).then_inc(ev["wT_ps"], 1)
                pe.wait_ge(ev["wT"], tile + 1)
                nc.tensor.matmul(ps_tile[:, 0:D], wT[:, :], be_sb[:, :], start=True, stop=True).then_inc(ev["b_ps"], 1)
                for n in range(E // 2):
                    if n == 0:
                        pe.wait_ge(ev["y0"], tile + 1)
                    else:
                        pe.wait_ge(y_step, tile * E + 2 * n)
                    for k in range(KT):
                        mm = nc.tensor.matmul(ps_tile[:, :], h2T[:, k, :], we_sb[k][:, 2 * n * D:2 * (n + 1) * D],
                                              start=(k == 0), stop=(k == KT - 1))
                    mm.then_inc(ev[f"e_ps{n}"], 1)

        @block.scalar
        def _(act):
            for t in range(TILES):
                act.wait_ge(h0T_ps, t + 1)
                for k, hT in enumerate((h0T, h0T2)):
                    cp = nc.scalar.copy(hT[:, t * P:(t + 1) * P], ps_front[:, t % 2, k * P:(k + 1) * P])
                cp.then_inc(h0T_rdy, 1)

            def steps(step):
                par = step.par
                for k in range(NCH):
                    if k == 2 and step.tail:
                        wait(act, pv_done, step, NCH, -NCH)
                        nc.scalar.copy(osb2[:, :, :], ps_out[:, :, 0:4 * OW]).then_inc(out_copied, 1)
                    if step.attend:
                        b = 1 - par
                        _, nn = keys_of(k)
                        slot = P_SLOT[b][k]
                        for e in range(2):
                            h = 2 * k + e
                            wait(act, score_done, step, 2 * NCH, h + 1 - 2 * NCH)
                            if e == 0:
                                wait(act, pv_done, step, NCH, P_PREV[b][k] + 1 - NCH)
                            nc.scalar.activation(prob[slot][0:nn, e * 512:e * 512 + 512],
                                                 ps_score[0:nn, S_BANK[h], :], ACT.Exp).then_inc(exp_done, 1)
                    if step.front:
                        for f in SLOTS[k]:
                            if f >= F_M and f < F_S:
                                continue
                            wait(act, front_done, step, NF, POS[f] + 1)
                            bank = ps_front[:, F_BANK[POS[f]], :]
                            if f < F_V:
                                t, n = divmod(f, NPIECE)
                                n0, nn = piece(n)
                                if n == 0:
                                    wait(act, k_stacked[t], step, 192, 0)
                                nc.scalar.activation(khigh[:, t, n0:n0 + nn], bank[:, 0:nn], ACT.Identity,
                                                     bias=bcol[:, 1, t:t + 1]).then_inc(high_done, 1)
                            elif f < F_M:
                                c0 = 2 * (f - F_V)
                                nch = min(2, NCH - c0)
                                rows = P if c0 + nch < NCH else LAST
                                if f == F_V:
                                    wait(act, pv_done, step, NCH, -NCH)
                                nc.scalar.copy(vstack[par][0:rows, c0:c0 + nch, :, 0:32],
                                               bank[0:rows, 0:nch * D].rearrange("p (c h d) -> p c h d", c=nch, h=HP))\
                                    .then_inc(high_done, 1)
                            else:
                                h0_ = 4 * (f - F_S)
                                nc.scalar.copy(qstack[par][96:98, h0_:h0_ + 4, :],
                                               bank[96:98, :].rearrange("p (h c) -> p h c", h=4)).then_inc(front_free, 1)

            run_steps(act, steps, B, B + 2)

            def evacuate(dst, n, need, done, tile):
                act.wait_ge(ev[need], tile + 1)
                nc.scalar.copy(dst, ps_tile[:, 0:n]).then_inc(ev[done], 1)

            flat = lambda a: a[:, :, :].rearrange("p a b -> p (a b)")
            with act.Fori(0, TILES) as tile:
                evacuate(flat(attT), D, "attT_ps", "attT", tile)
                evacuate(flat(h1T), D, "h1T_ps", "h1T", tile)
                evacuate(flat(qkT), 2 * D, "rT_ps", "rT", tile)
                for g in range(2):
                    act.wait_ge(ev[f"sub{g}"], tile + 1)
                    nc.scalar.activation(sc[:, g, :], sc[:, g, :], ACT.Exp).then_inc(ev["sexp"], 1) if g == 1 else \
                        nc.scalar.activation(sc[:, g, :], sc[:, g, :], ACT.Exp)
                for g in range(2):
                    evacuate(flat(pT)[:, g * 512:(g + 1) * 512], 512, f"pT_ps{g}", f"pT{g}", tile)
                evacuate(flat(att2T), D, "att2T_ps", "att2T", tile)
                evacuate(flat(h2T), D, "h2T_ps", "h2T", tile)
                act.wait_ge(ev["lneg"], tile + 1)
                nc.scalar.activation(ex[:, :], lg[:, :], ACT.Exp, bias=one1[:, 1:2], accum_out=one1[:, 2:3])\
                    .then_inc(ev["ex"], 1)
                act.wait_ge(ev["wT_ps"], tile + 1)
                nc.scalar.copy(wT[:, :], ps_tile[0:E, 0:P]).then_inc(ev["wT"], 1)

        @block.vector
        def _(dve):
            count = [0]

            def link(ins):
                count[0] += 1
                ins.then_inc(chain0, 1)
                dve.wait_ge(chain0, count[0])

            nc.vector.memset(kstack[0][96:98, :, :].rearrange("p a n -> p (a n)").bitcast(f32), ONES2).then_inc(fills_set, 1)
            for p in range(2):
                nc.vector.memset(vstack[p][:, :, :, 64:66], 1.0).then_inc(fills_set, 1)
            dve.wait_ge(ld_x, 16)
            for t in range(TILES):
                st = nc.vector.bn_stats(st0[:, t, :], x_all[:, t * D:(t + 1) * D])
            link(st)
            for t in range(TILES):
                ag = nc.vector.bn_aggr(mv0[:, t, :], st0[:, t, :])
            link(ag)
            nc.vector.tensor_scalar_add(ve0[:, :], mv0[:, :, 1], EPS).then_inc(ve0_rdy, 1)
            dve.wait_ge(ld_b, 16)
            nc.vector.tensor_scalar_mul(bq4[:, :], bcol[:, 0, :], DH ** -0.5)
            dve.wait_ge(ld_c, 16)
            nc.vector.tensor_copy(ident_bf[:, :], ident)
            dve.wait_ge(rs0_rdy, 1)
            for t in range(TILES):
                if t >= 4:
                    dve.wait_ge(h0T_ps, t - 3)
                nc.vector.tensor_scalar(h0[:, t % 4, :], x_all[:, t * D:(t + 1) * D], mv0[:, t, 0:1], rs0[:, t:t + 1],
                                        ALU.subtract, ALU.mult).then_inc(h0_rdy, 1)
            dve.wait_ge(ld_w, 32)
            for n in range(2):
                nc.vector.tensor_copy(w_hi[n][:, :, :], w_f[n][:, :, :]).then_inc(w_rdy, 1)
            dve.wait_ge(w_rdy, 2)
            for n in range(2):
                nc.vector.tensor_tensor(w_lo[n][:, :, :], w_f[n][:, :, :], w_hi[n][:, :, :], ALU.subtract)\
                    .then_inc(w_rdy, 1)
            for o in range(KT):
                for half in range(2):
                    dve.wait_ge(q_ps, 2 * o + half + 1)
                    last = nc.vector.tensor_scalar(
                        qT[o][:, half * 512:half * 512 + 512], ps_score[:, half, :] if o == 0 else ps_out[:, half, :],
                        DH ** -0.5, bq4[:, o:o + 1], ALU.mult, ALU.add)
            link(last)
            for o in range(KT):
                last = nc.vector.tensor_copy(qhi[o][:, :], qT[o][:, :])
            link(last)
            for o in range(KT):
                last = nc.vector.tensor_tensor(qlo[o][:, :], qT[o][:, :], qhi[o][:, :], ALU.subtract)
            link(last)
            for o in range(KT):
                for src, dst in ((qhi[o], qbd_hi), (qlo[o], qbd_lo)):
                    for j in range(2):
                        last = nc.vector.tensor_scalar(dst[:, :, o, j * SQ:(j + 1) * SQ],
                                                       src[:, :].rearrange("p (b q) -> p b q", b=B), jmask[:, j:j + 1], None,
                                                       ALU.mult)
                    last.then_inc(qbd_rdy, 1)
            dve.wait_ge(q_sent, 32)
            nc.vector.memset(kstack[1][96:98, :, :].rearrange("p a n -> p (a n)").bitcast(f32), ONES2).then_inc(fills_set, 1)
            nc.vector.memset(cum[:, :], 0.0).then_inc(ev["cum"], 1)
            for b in range(2):
                nc.vector.memset(vbd[b][:, :, :, :], 0.0).then_inc(fills_set, 1)

            def low_prob(step, k):
                b = 1 - step.par
                _, nn = keys_of(k)
                slot = P_SLOT[b][k]
                wait(dve, exp_done, step, 2 * NCH, 2 * k + 2 - 2 * NCH)
                wait(dve, pv_done, step, NCH, P_PREV[b][k] + 1 - NCH)
                nc.vector.tensor_tensor(plow[slot][0:nn, :], prob[slot][0:nn, :], p_high(slot, 0, HP * P)[0:nn],
                                        ALU.subtract).then_inc(plow_dve, 1)

            def steps(step):
                par = step.par
                for k in range(NCH):
                    if step.attend and k >= 1 and k - 1 in DVE_CHUNKS:
                        low_prob(step, k - 1)
                    if k == 3 and step.tail:
                        wait(dve, out_copied, step, 1, -1)
                        nc.vector.reciprocal(orec[:, :], osb[:, :, 64])
                        nc.vector.tensor_tensor(osum[:, :, :], osb[:, :, 0:32], osb[:, :, 32:64], ALU.add)\
                            .then_inc(out_summed, 1)
                        wait(dve, out_summed, step, 1, -1)
                        col = step.half(-1) * D
                        rows = slice(64 * par, 64 * par + 64)
                        for j in range(2):
                            half = slice(64 * j, 64 * j + 64)
                            dst = att_all[rows, bass.ds(col, D)] if step.i is not None else att_all[rows, col:col + D]
                            nc.vector.tensor_tensor(
                                dst.rearrange("p (h j d) -> p h j d", h=HP, j=2)[:, :, j, :],
                                osum[half, :, j * DH:(j + 1) * DH],
                                orec[half, :].unsqueeze(2).to_broadcast([64, HP, DH]), ALU.mult).then_inc(att_done, 1)
                    if step.front:
                        for f in SLOTS[k]:
                            bank = ps_front[:, F_BANK[POS[f]], :]
                            if f < F_M:
                                wait(dve, high_done, step, F_M, f + 1)
                            elif f < F_S:
                                wait(dve, front_done, step, NF, POS[f] + 1)
                            if f < F_V:
                                t, n = divmod(f, NPIECE)
                                n0, nn = piece(n)
                                if n == 0:
                                    wait(dve, k_stacked[t], step, 192, 0)
                                nc.vector.scalar_tensor_tensor(klow[:, t, n0:n0 + nn], bank[:, 0:nn], bcol[:, 1, t:t + 1],
                                                               khigh[:, t, n0:n0 + nn], ALU.add, ALU.subtract)\
                                    .then_inc(front_free, 1)
                            elif f < F_M:
                                c0 = 2 * (f - F_V)
                                nch = min(2, NCH - c0)
                                rows = P if c0 + nch < NCH else LAST
                                v = vstack[par][0:rows, c0:c0 + nch, :, :]
                                nc.vector.tensor_tensor(v[:, :, :, 32:64],
                                                        bank[0:rows, 0:nch * D].rearrange("p (c h d) -> p c h d", c=nch, h=HP),
                                                        v[:, :, :, 0:32], ALU.subtract).then_inc(front_free, 1)
                            elif f < F_S:
                                hp, n = divmod(f - F_M, NPIECE)
                                _, nn = piece(n)
                                nc.vector.reduce_max(maxes[:, hp, n:n + 1], bank[:, 0:nn], AX.X).then_inc(front_free, 1)
                                if f == F_S - 1:
                                    wait(dve, front_free, step, NF, F_S)
                                    nc.vector.tensor_reduce(negmax[:, :], maxes[:, :, :], AX.X, ALU.max, negate=True)\
                                        .then_inc(max_done, 1)
                                    wait(dve, max_done, step, 2, 1)
                                    nc.vector.tensor_copy(mparts[:, :, 0], negmax[:, :]).then_inc(max_done, 1)
                                    wait(dve, max_done, step, 2, 2)
                                    nc.vector.tensor_tensor(mparts[:, :, 1], negmax[:, :], mparts[:, :, 0], ALU.subtract)\
                                        .then_inc(shift_ready, 1)

            run_steps(dve, steps, B, B + 2)

            def tt(out_, a, b, op, done, tile, need=(), back=False):
                for n in need:
                    dve.wait_ge(ev[n], tile + 1)
                nc.vector.tensor_tensor(out_, a, b, op).then_inc(ev[done], 1)

            def normalise(n, src, dst, src_ev, tile, between):
                a = n + 1
                dve.wait_ge(ev[src_ev], tile + 1)
                nc.vector.bn_stats(stats[:, n, :], src[:, :]).then_inc(ev[f"st{a}"], 1)
                dve.wait_ge(ev[f"st{a}"], tile + 1)
                between()
                nc.vector.bn_aggr(mv[:, n, :], stats[:, n, :]).then_inc(ev[f"ag{a}"], 1)
                dve.wait_ge(ev[f"ag{a}"], tile + 1)
                nc.vector.tensor_scalar_add(ve[:, n:n + 1], mv[:, n, 1:2], EPS).then_inc(ev[f"ve{a}"], 1)
                dve.wait_ge(ev[f"rs{a}"], tile + 1)
                nc.vector.tensor_scalar(dst[:, :], src[:, :], mv[:, n, 0:1], rs[:, n:n + 1], ALU.subtract, ALU.mult)\
                    .then_inc(ev[f"h{a}"], 1)

            dve.wait_ge(ld_t, 16 * 6)
            dve.wait_ge(att_done, 2 * B)
            with dve.Fori(0, TILES) as tile:
                col = tile * D
                tt(att_b[:, :], att_all[:, bass.ds(col, D)], brow[:, 0, :], ALU.add, "att_b", tile)
                tt(xb[:, :], x_all[:, bass.ds(col, D)], brow[:, 1, :], ALU.add, "xb", tile)
                tt(x1[:, :], ps_tile[:, 0:D], xb[:, :], ALU.add, "x1", tile, ("o_ps", "xb"))
                normalise(0, x1, h1, "x1", tile, lambda: tt(x2b[:, :], x1[:, :], brow[:, 5, :], ALU.add, "x1b", tile))
                tt(qk[:, :], ps_tile[:, :], brow[:, 2:4, :].rearrange("p a n -> p (a n)"), ALU.add, "qk", tile, ("qk_ps",))
                dve.wait_ge(ev["v_ps"], tile + 1)
                for b in range(2):
                    rows = slice(64 * b, 64 * b + 64)
                    for j in range(2):
                        vin = ps_tile[rows, 0:D].rearrange("p (h j d) -> p h j d", h=HP, j=2)[:, :, j, :]
                        bin_ = brow[rows, 4, :].rearrange("p (h j d) -> p h j d", h=HP, j=2)[:, :, j, :]
                        last = nc.vector.tensor_tensor(vbd[b][64 * j:64 * j + 64, :, j, :], vin, bin_, ALU.add)
                last.then_inc(ev["v"], 1)
                qh = qk[:, :].rearrange("p (h d) -> p h d", d=DH)
                rh = rot[:, :].rearrange("p (h d) -> p h d", d=DH)
                tt(rh[:, :, 0:8], qh[:, :, 0:8], qh[:, :, 1:DH:2], ALU.subtract, "rotA", tile, ("qk",))
                tt(rh[:, :, 8:DH], qh[:, :, 8:DH], qh[:, :, 0:DH:2], ALU.add, "rotB", tile)
                dve.wait_ge(ev["rotA"], tile + 1)
                dve.wait_ge(ev["rotB"], tile + 1)
                for a in range(2):
                    part = rot[:, a * D:(a + 1) * D].rearrange("p (h d) -> p h d", d=DH)
                    tab = rope[:, a * DH:(a + 1) * DH].unsqueeze(1).to_broadcast([P, HEADS, DH])
                    last = nc.vector.tensor_tensor(part, part, tab, ALU.mult)
                last.then_inc(ev["rot"], 1)
                dve.wait_ge(ev["rT"], tile + 1)
                for g in range(2):
                    for b in range(2):
                        last = nc.vector.tensor_tensor(
                            kbd[:, g, b, :].rearrange("p (h k) -> p h k", h=8),
                            qkT[:, 2 + g, 64 * b:64 * b + 64].unsqueeze(1).to_broadcast([P, 8, SQ]),
                            mask8.unsqueeze(2).to_broadcast([P, 8, SQ]), ALU.mult)
                last.then_inc(ev["kbd"], 1)
                for g in range(2):
                    sview = ps_tile[:, :].rearrange("p (h k) -> p h k", h=8)
                    dve.wait_ge(ev[f"s_ps{g}"], tile + 1)
                    nc.vector.reduce_max(smax[:, 8 * g:8 * g + 8], sview, AX.X).then_inc(ev[f"smax{g}"], 1)
                    tt(sc[:, g, :].rearrange("p (h k) -> p h k", h=8), sview,
                       smax[:, 8 * g:8 * g + 8].unsqueeze(2).to_broadcast([P, 8, SQ]), ALU.subtract, f"sub{g}", tile,
                       (f"smax{g}",))
                dve.wait_ge(ev["sexp"], tile + 1)
                nc.vector.reduce_sum(ssum[:, :], sc[:, :, :].rearrange("p g (h k) -> p (g h) k", h=8), AX.X)\
                    .then_inc(ev["ssum"], 1)
                dve.wait_ge(ev["ssum"], tile + 1)
                nc.vector.reciprocal(srec[:, :], ssum[:, :]).then_inc(ev["srec"], 1)
                tt(att2[:, :].rearrange("p (h d) -> p h d", d=DH), ps_tile[:, 0:D].rearrange("p (h d) -> p h d", d=DH),
                   srec[:, :].unsqueeze(2).to_broadcast([P, HEADS, DH]), ALU.mult, "att2", tile, ("pv_ps", "srec"))
                tt(x2[:, :], ps_tile[:, 0:D], x2b[:, :], ALU.add, "x2", tile, ("w_ps", "x1b"))
                normalise(1, x2, h2, "x2", tile, lambda: nc.vector.tensor_copy(one1[:, 0:1], x2[:, 0:1]))
                dve.wait_ge(ev["lg_ps"], tile + 1)
                nc.vector.tensor_copy(lg[:, :], ps_tile[:, 0:E]).then_inc(ev["lg"], 1)
                dve.wait_ge(ev["lg"], tile + 1)
                nc.vector.reduce_max(one1[:, 0:1], lg[:, :], AX.X).then_inc(ev["lmax"], 1)
                dve.wait_ge(ev["lmax"], tile + 1)
                nc.vector.tensor_scalar_mul(one1[:, 1:2], one1[:, 0:1], -1.0).then_inc(ev["lneg"], 1)
                nc.vector.scalar_tensor_tensor(eq[:, :], lg[:, :], one1[:, 0:1], desc, ALU.is_equal, ALU.mult)\
                    .then_inc(ev["eqd"], 1)
                dve.wait_ge(ev["eqd"], tile + 1)
                nc.vector.reduce_max(one1[:, 3:4], eq[:, :], AX.X).then_inc(ev["eqm"], 1)
                dve.wait_ge(ev["eqm"], tile + 1)
                nc.vector.tensor_scalar(mask[:, :], desc, one1[:, 3:4], None, ALU.is_equal).then_inc(ev["mask"], 1)
                dve.wait_ge(ev["ex"], tile + 1)
                nc.vector.reciprocal(one1[:, 4:5], one1[:, 2:3]).then_inc(ev["gate"], 1)
                dve.wait_ge(ev["loc_ps"], tile + 1)
                dve.wait_ge(ev["mask"], tile + 1)
                nc.vector.scalar_tensor_tensor(keep[:, :], ps_tile[:, 0:E], float(CAP), mask[:, :], ALU.is_lt, ALU.mult)\
                    .then_inc(ev["keep"], 1)
                tt(cum[:, :], cum[:, :], mask[:, :], ALU.add, "cum", tile)
                dve.wait_ge(ev["keep"], tile + 1)
                dve.wait_ge(ev["gate"], tile + 1)
                nc.vector.tensor_scalar(wgt[:, :], keep[:, :], one1[:, 4:5], None, ALU.mult).then_inc(ev["wgt"], 1)
                dve.wait_ge(ev["out"], tile * 16 + 16)
                tt(y[:, :], ps_tile[:, 0:D], x2[:, :], ALU.add, "y0", tile, ("b_ps",))
                dve.wait_ge(ev["y0"], tile + 1)
                for n in range(E):
                    if n % 2 == 0:
                        dve.wait_ge(ev[f"e_ps{n // 2}"], tile + 1)
                    if n:
                        dve.wait_ge(y_step, tile * E + n)
                    last = nc.vector.scalar_tensor_tensor(y[:, :], ps_tile[:, (n % 2) * D:(n % 2 + 1) * D], wgt[:, n:n + 1],
                                                          y[:, :], ALU.mult, ALU.add).then_inc(y_step, 1)
                dve.wait_ge(y_step, tile * E + E)
                nc.vector.tensor_copy(one1[:, 5:6], y[:, 0:1]).then_inc(ev["y"], 1)


_INS = ["x", "ctxT", "wqT", "wkT", "wvT", "bqk", "woT", "wqkv", "wout", "brows", "wg", "weT", "be", "consts"]


def shape_constants():
    c = np.zeros((P, NCONST), np.float32)
    p = np.arange(P)
    c[:, C_ID:C_ID + P] = np.eye(P)
    c[:, C_TRI:C_TRI + P] = p[:, None] < p[None, :]
    c[:, C_MASK:C_MASK + 8] = (p[:, None] // DH) == np.arange(8)[None, :]
    c[:, C_J:C_J + 2] = (p[:, None] // DH % 2) == np.arange(2)[None, :]
    c[:, C_DESC:C_DESC + E] = E - np.arange(E)
    theta = np.float32(10000.0) ** (-np.arange(0, DH, 2, dtype=np.float32) / np.float32(DH))
    freqs = (p % SQ).astype(np.float32)[:, None] * theta[None, :]
    table = np.concatenate([np.sin(freqs), np.cos(freqs)], axis=-1).astype(np.float32)
    c[:, C_ROPE:C_ROPE + DH] = table * np.float32(DH ** -0.5)
    c[:, C_ROPE + DH:] = table
    return c


def kernel(**inputs):
    import numpy as _np
    import concourse.bacc as _bacc
    from concourse import mybir as _mybir
    from concourse.bass_utils import run_bass_kernel_spmd as _run

    a = {k: _np.asarray(v) for k, v in inputs.items()}
    t = lambda v, *axes: _np.ascontiguousarray(_np.transpose(v, axes))
    arrays = {
        "x": a["x"].reshape(B * SQ, D), "ctxT": t(a["ctx_1024"], 0, 2, 1),
        "wqT": t(a["L0_xattn_Wq"], 1, 0),
        "wkT": t(a["L0_xattn_Wk"], 1, 0),
        "wvT": t(a["L0_xattn_Wv"], 1, 0),
        "woT": t(a["L0_xattn_Wo"], 1, 0),
        "wqkv": a["L0_attn_Wqkv"], "wout": a["L0_attn_Wout"],
        "wg": a["L0_ffn_wg"], "weT": t(a["L0_ffn_W"], 0, 2, 1), "be": a["L0_ffn_b"], "consts": shape_constants(),
        "bqk": t(_np.stack([a["L0_xattn_bq"], a["L0_xattn_bk"]]).reshape(2, KT, P), 2, 0, 1),
        "brows": _np.concatenate([a["L0_xattn_bv"], a["L0_xattn_bo"], a["L0_attn_bqkv"], a["L0_attn_bout"]]),
    }
    nc = _bacc.Bacc("TRN2", target_bir_lowering=False, num_devices=1)
    args, ins = [], {}
    for name in _INS:
        v = _np.ascontiguousarray(arrays[name])
        ins[f"in_{name}"] = v
        args.append(nc.dram_tensor(f"in_{name}", v.shape, _mybir.dt.from_np(v.dtype), kind="ExternalInput").ap())
    args.append(nc.dram_tensor("out_0", (B * SQ, D), _mybir.dt.float32, kind="ExternalOutput").ap())
    build(nc, *args)
    r = _run(nc, [ins], core_ids=[0])
    return r.results[0]["out_0"].reshape(B, SQ, D)
```

```python
import numpy as np
import concourse.bass as bass
from concourse import mybir
from contextlib import ExitStack

P = 128
D = 256
KT = D // P
HEADS = 16
DH = D // HEADS
B = 16
SQ = 64
SK = 1601
NCH = -(-SK // P)
SKP = SK + SK % 2
LAST = SK - (NCH - 1) * P
HP = HEADS // 2
TILES = B * SQ // P
E = 8
CAP = B * SQ // E
EPS = 1e-5
VW = 66
OW = 65
NPAR = 4
NSB = 2
QSENT = 16 * 3 * 4
LANES = 4

C_ID, C_TRI, C_MASK, C_J, C_DESC, C_ROPE = 0, 128, 256, 264, 266, 274
NCONST = C_ROPE + 2 * DH

NPIECE = -(-SK // 512)
KUNITS = KT * NPIECE
VUNITS = -(-NCH // 2)
NKV = KUNITS + VUNITS
FULL = SK // 512
MUNITS = 2 * (4 * FULL + 1)
NM = MUNITS + 2
KV_SLOTS = [[0, 1], [2, 3], [8, 9], [4], [5], [6, 10], [7], [11], [12], [13], [], [], [14]]
M_COUNT = [0, 0, 0, 2, 2, 2, 2, 4, 3, 3, 3, 2, 3]
M_SLOTS = [list(range(sum(M_COUNT[:k]), sum(M_COUNT[:k + 1]))) for k in range(NCH)]
PE_ORDER = '0mKmm1wWKm'
PE_FIRST = 'Km0mRKm1wWKm'
DVE_ORDER = 'mapmmmKK'
DVE_FIRST = 'KmmaKmpKm'
ACT_ORDER = '0KK1'
ACT_FIRST = "KR0K1K"
LOW_AT = [0, 0, 0, 1]
SHIFT_SLOT = 10
SHIFT_POS = [M_SLOTS[SHIFT_SLOT][0], NM - 1]


def max_unit(m):
    half, nth = divmod(m, 4 * FULL + 1)
    if nth < 4 * FULL:
        return [(0, 4 * half + nth // FULL, nth % FULL)]
    rest = SK - FULL * 512
    return [(j * rest, 4 * half + j, FULL) for j in range(4)]


def q_at(hp):
    return 2 * (hp % 4) + hp // 4


def front_pos(m):
    return m + (m >= SHIFT_POS[0])


KV_POS = {u: n for n, u in enumerate(u for slot in KV_SLOTS for u in slot)}
GPS_CHUNKS = [2, 4, 5, 6, 7, 8, 9, 10, 11, 12]
DVE_CHUNKS = [k for k in range(NCH) if k not in GPS_CHUNKS]
LAST_GPS = [0, 3, 6, 9, 12]
LAST_DVE = [k for k in range(NCH) if k not in LAST_GPS]


def piece(n):
    return n * 512, min(512, SK - n * 512)


def keys_of(k):
    return k * P, (P if k < NCH - 1 else LAST)


ONES2 = float(np.array([0x3F803F80], np.uint32).view(np.float32)[0])


class Step:

    def __init__(self, i, u):
        self.i, self.u, self.par = i, u, u % 2
        self.front = i is not None or u < B
        self.attend = i is not None or 1 <= u <= B
        self.tail = i is not None or u >= 2

    def at(self, n, c):
        return n * self.u + c if self.i is None else self.i * (2 * n) + (n * self.u + c)

    def half(self, c):
        return self.u // 2 + c if self.i is None else self.i + (self.u // 2 + c)


def low_chunks(step, back):
    last = step.i is None and step.u - back == B - 1
    return (LAST_GPS, LAST_DVE) if last else (GPS_CHUNKS, DVE_CHUNKS)


def wait(eng, sem, step, n, c):
    if step.i is None and n * step.u + c <= 0:
        return
    assert n * step.u + c > 0
    eng.wait_ge(sem, step.at(n, c))


def run_steps(eng, emit, upto, last):
    emit(Step(None, 0))
    emit(Step(None, 1))
    with eng.Fori(0, (upto - 2) // 2) as i:
        emit(Step(i, 2))
        emit(Step(i, 3))
    for u in range(upto, last):
        emit(Step(None, u))


def last_use(k, slots_now, slots_before):
    for j in range(k - 1, -1, -1):
        if slots_now[j] == slots_now[k]:
            return j
    n = len(slots_before)
    for j in range(n - 1, -1, -1):
        if slots_before[j] == slots_now[k]:
            return j - n
    raise ValueError(k)


S_BANK = [h % NSB for h in range(2 * NCH)]
P_SLOT = [[(k + par) % NPAR for k in range(NCH)] for par in range(2)]
S_PREV = [last_use(h, S_BANK, S_BANK) for h in range(2 * NCH)]
P_PREV = [[last_use(k, P_SLOT[par], P_SLOT[1 - par]) for k in range(NCH)] for par in range(2)]


def build(nc, x, ctxT, wqT, wkT, wvT, bqk, woT, wqkv, wout, brows, wg, weT, be, consts, ones2, out):
    f32, bf16 = mybir.dt.float32, mybir.dt.bfloat16
    ALU, ACT, AX = mybir.AluOpType, mybir.ActivationFunctionType, mybir.AxisListType
    ctx = ExitStack()
    with ctx:
        def sb(name, shape, dt=f32):
            return ctx.enter_context(nc.sbuf_tensor(name, shape, dt))

        def sem(name):
            return ctx.enter_context(nc.semaphore(name))

        cst = sb("cst", [P, NCONST])
        ident, tri = cst[:, C_ID:C_ID + P], cst[:, C_TRI:C_TRI + P]
        mask8, jmask = cst[:, C_MASK:C_MASK + 8], cst[:, C_J:C_J + 2]
        desc, rope = cst[:, C_DESC:C_DESC + E], cst[:, C_ROPE:C_ROPE + 2 * DH]
        ident_bf = sb("ident_bf", [P, P], bf16)
        ones_f = sb("ones_f", [P, P])
        half_neg = sb("half_neg", [P, TILES])
        x_all = sb("x_all", [P, TILES * D])
        att_all = sb("att_all", [P, TILES * D])
        cbuf = [sb(f"cbuf{p}", [P, KT, SK]) for p in range(2)]
        clow = [sb(f"clow{p}", [P, KT, SK], bf16) for p in range(2)]
        khigh = sb("khigh", [P, KT, SKP], bf16)
        klow = sb("klow", [P, KT, SKP], bf16)
        kstack = [sb(f"kstack{p}", [P, HP, SKP], bf16) for p in range(2)]
        vstack = [sb(f"vstack{p}", [P, NCH, HP, VW], bf16) for p in range(2)]
        qstack = [sb(f"qstack{p}", [P, HP, P], bf16) for p in range(2)]
        prob = [sb(f"prob{p}", [P, HP * P]) for p in range(NPAR)]
        plow = [sb(f"plow{p}", [P, HP * P], bf16) for p in range(NPAR)]
        maxes = sb("maxes", [P, HP, NPIECE])
        negmax = sb("negmax", [P, HP])
        mparts = sb("mparts", [P, HP, 2], bf16)
        osb2 = sb("osb", [P, 2, 4 * OW])
        osb = osb2[:, :, :].rearrange("p a (h c) -> p (a h) c", c=OW)
        osum = sb("osum", [P, HP, 2 * DH])
        orec = sb("orec", [P, HP])
        w_f = [att_all[:, n * KT * D:(n + 1) * KT * D].rearrange("p (k n) -> p k n", k=KT) for n in range(2)]
        w_hi = [sb(f"w_hi{n}", [P, KT, D], bf16) for n in range(2)]
        w_lo = [sb(f"w_lo{n}", [P, KT, D], bf16) for n in range(2)]
        bcol = sb("bcol", [P, 2, KT])
        bq4 = sb("bq4", [P, KT])

        wq_sb = prob[0][:, 0:KT * D].rearrange("p (k n) -> p k n", k=KT)
        h0 = prob[1][:, :].rearrange("p (t n) -> p t n", n=D)
        h0T = cbuf[1][:, 0, 0:0 + 1024]
        h0T2 = cbuf[1][:, 1, 0:0 + 1024]
        qT = [prob[2], prob[3]]
        qhi = [plow[0], plow[1]]
        qlo = [plow[2], plow[3]]
        qbd_hi = kstack[1][:, 0:4, :].rearrange("p a n -> p (a n)")[:, 0:B * 2 * P]\
            .rearrange("p (b t c) -> p b t c", b=B, t=KT)
        qbd_lo = kstack[1][:, 4:8, :].rearrange("p a n -> p (a n)")[:, 0:B * 2 * P]\
            .rearrange("p (b t c) -> p b t c", b=B, t=KT)
        q_dram = nc.dram_tensor("q_stacked", [B, 96, HP, P], bf16, kind="Internal").ap()
        st0 = sb("st0", [P, TILES, 6])
        mv0 = sb("mv0", [P, TILES, 2])
        ve0 = sb("ve0", [P, TILES])
        rs0 = sb("rs0", [P, TILES])

        wo_sb = sb("wo_sb", [P, KT, D])
        wqkv_sb = sb("wqkv_sb", [P, KT, 3 * D])
        wqkv_low = sb("wqkv_low", [P, KT, 3 * D], bf16)
        wout_sb = sb("wout_sb", [P, KT, D])
        wg_sb = sb("wg_sb", [P, KT, E])
        be_sb = sb("be_sb", [E, D])
        brow = sb("brow", [P, 6, D])
        we_sb = [cbuf[k][:, :, :].rearrange("p k n -> p (k n)")[:, 0:E * D] for k in range(KT)]
        flat3 = lambda a: a[:, :, :].rearrange("p a b -> p (a b)")
        we_low = [flat3(clow[k])[:, 0:E * D] for k in range(KT)]
        rooms = [flat3(kstack[p]).bitcast(f32) for p in range(2)]
        rooms += [vstack[p][:, :, :, :].rearrange("p c h n -> p (c h n)").bitcast(f32) for p in range(2)]
        rooms += [prob[p][:, :] for p in range(NPAR)] + [flat3(a).bitcast(f32) for a in (khigh, klow)]
        used = [0] * len(rooms)

        def carve(n):
            r = min(r for r in range(len(rooms)) if used[r] + n <= rooms[r].shape[1])
            used[r] += n
            return rooms[r][:, used[r] - n:used[r]]

        lanes = range(LANES)
        kbd_flat = [carve(4 * 512) for _ in lanes]
        kbd = [a.rearrange("p (g b n) -> p g b n", g=2, b=2) for a in kbd_flat]
        pT = [a[:, 0:HP * P].rearrange("p (h n) -> p h n", h=HP) for a in kbd_flat]
        sc = [carve(2 * 512).rearrange("p (g n) -> p g n", g=2) for _ in lanes]
        qk, rot = [carve(2 * D) for _ in lanes], [carve(2 * D) for _ in lanes]
        qkT = [carve(2 * D).rearrange("p (k n) -> p k n", k=4) for _ in lanes]
        vbd = [carve(2 * D).rearrange("p (b h j d) -> p b h j d", b=2, h=HP, j=2) for _ in lanes]
        rows_in = [carve(D) for _ in lanes]
        rows_T = [carve(D).rearrange("p (k n) -> p k n", k=KT) for _ in lanes]
        rows_high, rows_low = ([carve(D // 2).bitcast(bf16).rearrange("p (k n) -> p k n", k=KT) for _ in lanes]
                               for _ in range(2))
        x_a = [carve(D) for _ in lanes]
        x_b = [carve(D) for _ in lanes]

        def lane_tiles(name, shape):
            return [sb(f"{name}_{n}", shape) for n in lanes]

        smax, ssum, srec = (lane_tiles(n, [P, HEADS]) for n in ("smax", "ssum", "srec"))
        stats, mv, ve, rs = lane_tiles("stats", [P, 6]), lane_tiles("mv", [P, 2]), lane_tiles("ve", [P, 1]), \
            lane_tiles("rs", [P, 1])
        lg, ex, eq, mask, keep, wgt = (lane_tiles(n, [P, E]) for n in ("lg", "ex", "eq", "mask", "keep", "wgt"))
        before = lane_tiles("before", [P, E])
        lmax, lneg, lsum, first, gate, spare = (lane_tiles(n, [P, 1]) for n in
                                                ("lmax", "lneg", "lsum", "first", "gate", "spare"))
        wT = lane_tiles("wT", [E, P])

        ps_kv = ctx.enter_context(nc.psum_tensor("ps_kv", [P, 2, 512], f32))
        ps_front = ctx.enter_context(nc.psum_tensor("ps_front", [P, 2, 512], f32))
        ps_score = ctx.enter_context(nc.psum_tensor("ps_score", [P, NSB, 512], f32))
        ps_out = ctx.enter_context(nc.psum_tensor("ps_out", [P, 2, 512], f32))
        bank = [[pair[:, n, :] for n in range(2)] for pair in (ps_kv, ps_front, ps_score, ps_out)]

        ld_ones, qhi_rdy, qbd_hi_rdy = sem("ld_ones"), sem("qhi_rdy"), sem("qbd_hi_rdy")
        ld_x, ld_c, ld_w, ld_wq, ld_b, ld_t, ld_e = (
            sem(n) for n in ("ld_x", "ld_c", "ld_w", "ld_wq", "ld_b", "ld_t", "ld_e"))
        ones_set, chain0, ve0_rdy, rs0_rdy = (sem(n) for n in ("ones_set", "chain0", "ve0_rdy", "rs0_rdy"))
        fills_set = sem("fills_set")
        h0_rdy, h0T_ps, h0T_rdy, q_ps, q_rdy, qbd_rdy, q_sent, w_rdy = (
            sem(n) for n in ("h0_rdy", "h0T_ps", "h0T_rdy", "q_ps", "q_rdy", "qbd_rdy", "q_sent", "w_rdy"))
        c_loaded = [sem("c_loaded0"), sem("c_loaded1")]
        q_loaded = sem("q_loaded")
        k_stacked = [sem(f"k_stacked{hp}") for hp in range(HP)]
        clow_done = sem("clow_done")
        kv_done, kv_free, high_done = sem("kv_done"), sem("kv_free"), sem("high_done")
        m_done, m_free = sem("m_done"), sem("m_free")
        max_done, shift_ready, shift_done, shift_copied = (
            sem(n) for n in ("max_done", "shift_ready", "shift_done", "shift_copied"))
        score_done, exp_done, pv_done = sem("score_done"), sem("exp_done"), sem("pv_done")
        plow_dve, plow_gps = sem("plow_dve"), sem("plow_gps")
        out_copied, out_summed, att_done = sem("out_copied"), sem("out_summed"), sem("att_done")

        ev = {n: sem("t_" + n) for n in (
            "att_b", "attT_ps", "attT", "o_ps", "xb", "x1", "stats1", "agg1", "var1", "rs1", "x_b",
            "h1", "h1T_ps", "h1T", "h1H", "h1L", "qk_ps", "qk", "v_ps", "v", "rotA", "rotB", "rot",
            "rT_ps", "rT", "kbd", "s_ps0", "s_ps1", "smax0", "smax1", "sub0", "sub1", "exp",
            "ssum", "srec", "pT_ps0", "pT_ps1", "pT", "pv_ps", "att2", "att2T_ps", "att2T",
            "w_ps", "x2", "stats2", "agg2", "var2", "rs2", "h2", "h2T_ps", "h2T", "h2H", "h2L",
            "lg_ps", "lg", "lmax", "lneg", "ranked", "first", "mask", "ex", "gate", "loc_ps",
            "keep", "before", "wgt", "wT_ps", "wT", "b_ps", "y0", "y", "out")}
        e_ps = [sem(f"t_e_ps{n}") for n in range(E // 2)]
        wqkv_rdy, we_rdy = sem("t_wqkv_rdy"), sem("t_we_rdy")
        y_step = [sem(f"t_y_step{n}") for n in lanes]

        def added(group, n):
            return group * E + n

        locations = lambda n: bank[n][1][:, 0:E]
        weights_T = lambda n: bank[n][1][0:E, P:2 * P]
        biases = lambda n: bank[n][1][:, D:2 * D]

        def values(eng, group, ahead=0):
            due = [group * LANES + (n + 1 + ahead) for n in lanes]
            return due if isinstance(group, int) else [eng.snap(value) for value in due]

        block = ctx.enter_context(nc.Block())

        def high(a):
            return a.bitcast(bf16)[:, 1::2]

        def kv_bank(step, u):
            return ps_kv[:, (KV_POS[u] + NKV * step.par) % 2, :]

        def c_high(par, k, n0, n):
            return cbuf[par][:, k, :].bitcast(bf16)[:, 2 * n0 + 1:2 * (n0 + n):2]

        def p_high(slot, c0, n):
            return prob[slot][:, :].bitcast(bf16)[:, 2 * c0 + 1:2 * (c0 + n):2]

        @block.sync
        def _(sp):
            sp.dma_start(x_all[:, :].rearrange("p (t d) -> p t d", t=TILES),
                         x.rearrange("(t p) d -> p t d", p=P)).then_inc(ld_x, 16)
            sp.dma_start(wq_sb, wqT.rearrange("(k p) n -> p k n", p=P)).then_inc(ld_wq, 16)
            sp.dma_start(cbuf[0][:, :, :], ctxT[0].rearrange("(k p) n -> p k n", p=P)).then_inc(c_loaded[0], 16)

            def steps(step):
                par = step.par
                now, nxt = step.at(1, 0), step.at(1, 2)
                wait(sp, score_done, step, 2 * NCH, -2 * NCH)
                src = q_dram[bass.ds(now, 1)] if step.i is not None else q_dram[step.u:step.u + 1]
                sp.dma_start(qstack[par][0:96, :, :], src[0]).then_inc(q_loaded, 16)
                for t in range(KT):
                    wait(sp, kv_free, step, NKV, KV_POS[NPIECE * (t + 1) - 1] + 1)
                    for r in range(4):
                        for g, src in enumerate((khigh, klow, khigh)):
                            sp.dma_start(kstack[par][32 * g:32 * g + 32, 4 * t + r, 0:SK],
                                         src[32 * r:32 * r + 32, t, 0:SK]).then_inc(k_stacked[4 * t + r], 16)
                if step.i is not None or step.u + 2 < B:
                    wait(sp, kv_done, step, NKV, NKV)
                    src = ctxT[nxt] if step.i is None else ctxT[bass.ds(nxt, 1)][0]
                    sp.dma_start(cbuf[par][:, :, :], src.rearrange("(k p) n -> p k n", p=P))\
                        .then_inc(c_loaded[par], 16)

            sp.dma_start(kstack[0][96:98, :, :].rearrange("p a n -> p (a n)").bitcast(f32), ones2).then_inc(ld_ones, 16)
            sp.wait_ge(q_ps, 4)
            sp.dma_start(cbuf[1][:, :, :], ctxT[1].rearrange("(k p) n -> p k n", p=P)).then_inc(c_loaded[1], 16)
            sp.wait_ge(qbd_hi_rdy, 2)
            for g, parts in enumerate((qbd_hi, qbd_hi, qbd_lo)):
                if g == 2:
                    sp.wait_ge(qbd_rdy, 2)
                for r in range(4):
                    sp.dma_start(q_dram[:, 32 * g:32 * g + 32, 2 * r:2 * r + 2, :].rearrange("b q t c -> q b (t c)"),
                                 parts[32 * r:32 * r + 32, :, :, :].rearrange("q b t c -> q b (t c)")).then_inc(q_sent, 16)
            sp.wait_ge(q_sent, QSENT)
            sp.dma_start(kstack[1][96:98, :, :].rearrange("p a n -> p (a n)").bitcast(f32), ones2).then_inc(ld_ones, 16)
            run_steps(sp, steps, B - 2, B)
            sp.wait_ge(kv_done, NKV * B)
            for k in range(KT):
                sp.dma_start(we_sb[k].rearrange("p (e n) -> p e n", e=E),
                             weT.rearrange("e (k p) n -> k p e n", p=P)[k]).then_inc(ev["out"] if k else ld_e, 16)
            with sp.Fori(0, TILES // LANES) as group:
                due = values(sp, group)
                for n in lanes:
                    row = sp.snap(group * (LANES * P) + n * P)
                    sp.wait_ge(ev["y"], due[n])
                    sp.wait_ge(ld_x, 16)
                    sp.dma_start(out[bass.ds(row, P), :], x_b[n]).then_inc(ev["out"], 16)
            sp.wait_ge(ev["out"], 16 * TILES + 16)
        @block.gpsimd
        def _(pool):
            nc.gpsimd.memset(ones_f[:, :], 1.0).then_inc(ones_set, 1)
            nc.gpsimd.memset(half_neg[:, :], -0.5).then_inc(ones_set, 1)
            pool.dma_start(cst[:, :], consts).then_inc(ld_c, 16)
            pool.dma_start(w_f[0][:, :, :], wkT.rearrange("(k p) n -> p k n", p=P)).then_inc(ld_w, 16)
            pool.dma_start(w_f[1][:, :, :], wvT.rearrange("(k p) n -> p k n", p=P)).then_inc(ld_w, 16)
            pool.dma_start(bcol[:, :, :], bqk).then_inc(ld_b, 16)
            pool.wait_ge(ones_set, 2)
            pool.wait_ge(ve0_rdy, 1)
            nc.gpsimd.tensor_tensor(rs0[:, :], ve0[:, :], half_neg[:, :], ALU.pow).then_inc(rs0_rdy, 1)
            pool.dma_start(wo_sb[:, :, :], woT.rearrange("(k p) n -> p k n", p=P)).then_inc(ld_t, 16)
            pool.dma_start(wqkv_sb[:, :, :], wqkv.rearrange("(k p) n -> p k n", p=P)).then_inc(ld_t, 16)
            pool.dma_start(wout_sb[:, :, :], wout.rearrange("(k p) n -> p k n", p=P)).then_inc(ld_t, 16)
            pool.dma_start(wg_sb[:, :, :], wg.rearrange("(k p) n -> p k n", p=P)).then_inc(ld_t, 16)
            pool.dma_start(be_sb[:, :], be).then_inc(ld_t, 16)
            pool.dma_start(brow[:, :, :].rearrange("p a n -> p (a n)"), brows.partition_broadcast(P)).then_inc(ld_t, 16)
            def low_context(par, quarter):
                for k in (quarter // 2,):
                    for a, n in (((0, 801), (801, 800))[quarter % 2],):
                        nc.gpsimd.tensor_tensor(clow[par][:, k, a:a + n], cbuf[par][:, k, a:a + n],
                                                c_high(par, k, a, n), ALU.subtract).then_inc(clow_done, 1)

            pool.wait_ge(c_loaded[0], 16)
            for quarter in range(4):
                low_context(0, quarter)
            pool.wait_ge(ld_t, 16 * 6)
            for k in range(KT):
                nc.gpsimd.tensor_tensor(wqkv_low[:, k, :], wqkv_sb[:, k, :], high(wqkv_sb[:, k, :]), ALU.subtract)\
                    .then_inc(wqkv_rdy, 1)

            def steps(step):
                par = step.par
                if step.i is not None or step.u + 1 < B:
                    pool.wait_ge(c_loaded[1 - par], ctx_value(step))
                    wait(pool, kv_done, step, NKV, 0)
                    for quarter in range(4):
                        if LOW_AT[quarter] == 0 or not step.attend:
                            low_context(1 - par, quarter)
                if step.attend:
                    b = 1 - par
                    for nth, k in enumerate(low_chunks(step, 1)[0]):
                        if step.i is not None or step.u + 1 < B:
                            for quarter in range(4):
                                if nth and LOW_AT[quarter] == nth:
                                    low_context(1 - par, quarter)
                        _, n = keys_of(k)
                        slot = P_SLOT[b][k]
                        wait(pool, exp_done, step, 2 * NCH, 2 * k + 2 - 2 * NCH)
                        wait(pool, pv_done, step, NCH, P_PREV[b][k] + 1 - NCH)
                        nc.gpsimd.tensor_tensor(plow[slot][0:n, :], prob[slot][0:n, :], p_high(slot, 0, HP * P)[0:n],
                                                ALU.subtract).then_inc(plow_gps, 1)

            def ctx_value(step):
                if step.i is None:
                    return 16 * ((step.u + 1) // 2 + 1)
                return step.i * 16 + 16 * ((step.u + 1) // 2 + 1)

            run_steps(pool, steps, B - 2, B + 2)
            def inverse_root(n, a, due):
                pool.wait_ge(ev["var" + a], due[n])
                nc.gpsimd.tensor_tensor(rs[n][:, :], ve[n][:, :], half_neg[:, 0:1], ALU.pow).then_inc(ev["rs" + a], 1)

            def low_rows(n, a, due):
                pool.wait_ge(ev[f"h{a}H"], due[n])
                nc.gpsimd.tensor_tensor(flat3(rows_low[n]), flat3(rows_T[n]), flat3(rows_high[n]), ALU.subtract)\
                    .then_inc(ev[f"h{a}L"], 1)

            def group_work(group):
                due = values(pool, group)
                for dst, src, row, done in ((rows_in, att_all, 0, "att_b"), (x_a, x_all, 1, "xb")):
                    for n in lanes:
                        pool.wait_ge(ev["y0"], due[n])
                        col = group * (LANES * D) + n * D
                        if isinstance(group, int):
                            rows = src[:, col:col + D]
                        else:
                            rows = src[:, bass.ds(pool.snap(col), D)]
                        nc.gpsimd.tensor_tensor(dst[n], rows, brow[:, row, :], ALU.add).then_inc(ev[done], 1)
                for n in lanes:
                    inverse_root(n, "1", due)
                for n in lanes:
                    low_rows(n, "1", due)
                pool.wait_ge(ev["out"], group * (16 * LANES) + 16)
                for n in lanes:
                    pool.wait_ge(ev["x1"], due[n])
                    nc.gpsimd.tensor_tensor(x_b[n], x_a[n], brow[:, 5, :], ALU.add).then_inc(ev["x_b"], 1)
                if isinstance(group, int):
                    pool.wait_ge(ld_e, 16)
                    for k in range(KT):
                        for a in range(0, E * D, 4 * D):
                            nc.gpsimd.tensor_tensor(we_low[k][:, a:a + 4 * D], we_sb[k][:, a:a + 4 * D],
                                                    high(we_sb[k][:, a:a + 4 * D]), ALU.subtract).then_inc(we_rdy, 1)
                for n in lanes:
                    inverse_root(n, "2", due)
                for n in lanes:
                    low_rows(n, "2", due)

            group_work(0)
            with pool.Fori(1, TILES // LANES) as group:
                group_work(group)

        @block.tensor
        def _(pe):
            pe.wait_ge(ld_c, 16)
            for t in range(TILES):
                pe.wait_ge(h0_rdy, t + 1)
                if t >= 2:
                    pe.wait_ge(h0T_rdy, t - 1)
                for k in range(KT):
                    mm = nc.tensor.transpose(ps_front[:, t % 2, k * P:(k + 1) * P],
                                             h0[:, t % 4, k * P:(k + 1) * P], ident)
                mm.then_inc(h0T_ps, 1)
            pe.wait_ge(ld_wq, 16)
            pe.wait_ge(h0T_rdy, TILES)
            for o in range(KT):
                for half in range(2):
                    for k, hT in enumerate((h0T, h0T2)):
                        mm = nc.tensor.matmul(ps_score[:, half, :] if o == 0 else ps_out[:, half, :],
                                              wq_sb[:, k, o * P:(o + 1) * P], hT[:, half * 512:half * 512 + 512],
                                              start=(k == 0), stop=(k == KT - 1))
                    mm.then_inc(q_ps, 1)
            pe.wait_ge(w_rdy, 4)

            def project(step, u):
                par = step.par
                wait(pe, kv_free, step, NKV, KV_POS[u] - 1)
                ps = kv_bank(step, u)
                if u < KUNITS:
                    t, n = divmod(u, NPIECE)
                    n0, nn = piece(n)
                    terms = [(w, c, k) for k in range(KT) for w, c in ((w_hi, 0), (w_hi, 1), (w_lo, 0))]
                    for j, (w, c, k) in enumerate(terms):
                        rhs = clow[par][:, k, n0:n0 + nn] if c else c_high(par, k, n0, nn)
                        mm = nc.tensor.matmul(ps[:, 0:nn], w[0][:, k, t * P:(t + 1) * P], rhs,
                                              start=(j == 0), stop=(j == len(terms) - 1))
                else:
                    c0 = 2 * (u - KUNITS)
                    for a, c in enumerate(range(c0, min(c0 + 2, NCH))):
                        n0, nn = keys_of(c)
                        terms = [(w, hi, k) for k in range(KT) for w, hi in ((w_hi, 1), (w_lo, 1), (w_hi, 0))]
                        for j, (w, hi, k) in enumerate(terms):
                            lhs = c_high(par, k, n0, nn) if hi else clow[par][:, k, n0:n0 + nn]
                            mm = nc.tensor.matmul(ps[0:nn, a * D:(a + 1) * D], lhs, w[1][:, k, :],
                                                  start=(j == 0), stop=(j == len(terms) - 1))
                mm.then_inc(kv_done, 1)

            def max_scores(step, m):
                par = step.par
                ps = ps_front[:, front_pos(m) % 2, :]
                bank_free(step, front_pos(m))
                if m == 0:
                    wait(pe, q_loaded, step, 16, 16)
                for at, hp, n in max_unit(m):
                    n0, nn = piece(n)
                    if n == 0:
                        wait(pe, k_stacked[hp], step, 48, 48)
                    mm = nc.tensor.matmul(ps[:, at:at + nn], qstack[par][0:96, q_at(hp), :],
                                          kstack[par][0:96, hp, n0:n0 + nn], start=True, stop=True)
                mm.then_inc(m_done, 1)

            def bank_free(step, pos, back=0):
                pos, back = (pos - 2, back) if pos >= 2 else (pos - 2 + NM, back + 1)
                if pos in SHIFT_POS:
                    wait(pe, shift_copied, step, 2, SHIFT_POS.index(pos) + 1 - 2 * back)
                else:
                    wait(pe, m_free, step, MUNITS, pos - (pos > SHIFT_POS[0]) + 1 - MUNITS * back)

            def shift_rows(step, half, back):
                wait(pe, shift_ready, step, 2, half + 1 - 2 * back)
                bank_free(step, SHIFT_POS[half], back)
                for j in range(4):
                    mm = nc.tensor.matmul(ps_front[96:98, SHIFT_POS[half] % 2, j * P:(j + 1) * P],
                                          mparts[:, 4 * half + j, :], ident_bf[:, :], start=True, stop=True,
                                          tile_position=(0, 96))
                mm.then_inc(shift_done, 1)

            def score_half(step, h):
                k, e = divmod(h, 2)
                n0, nn = keys_of(k)
                par = 1 - step.par
                wait(pe, exp_done, step, 2 * NCH, S_PREV[h] + 1 - 2 * NCH)
                if k == 0:
                    wait(pe, shift_copied, step, 2, e - 1)
                for j in range(4):
                    hp = 4 * e + j
                    mm = nc.tensor.matmul(ps_score[0:nn, S_BANK[h], j * P:(j + 1) * P],
                                          kstack[par][0:98, hp, n0:n0 + nn], qstack[par][0:98, q_at(hp), :],
                                          start=True, stop=True)
                mm.then_inc(score_done, 1)

            def weigh(step, k, back, half):
                b = (step.par + back) % 2
                n0, nn = keys_of(k)
                slot = P_SLOT[b][k]
                if half == 0:
                    gps, dve = low_chunks(step, back)
                    if k in gps:
                        wait(pe, plow_gps, step, len(GPS_CHUNKS), gps.index(k) + 1 - back * len(GPS_CHUNKS))
                    else:
                        wait(pe, plow_dve, step, len(DVE_CHUNKS), dve.index(k) + 1 - back * len(DVE_CHUNKS))
                    if k == 0:
                        wait(pe, out_copied, step, 1, -back)
                for hp in range(4 * half, 4 * half + 4):
                    o = ps_out[:, half, (hp % 4) * OW:(hp % 4 + 1) * OW]
                    for part in range(2):
                        lhs = plow[slot][0:nn, hp * P:(hp + 1) * P] if part else p_high(slot, hp * P, P)[0:nn]
                        mm = nc.tensor.matmul(o, lhs, vstack[b][0:nn, k, hp, 0:OW],
                                              start=(k == 0 and part == 0 and hp % 4 == 0),
                                              stop=(k == NCH - 1 and part == 1 and hp % 4 == 3),
                                              skip_group_check=True)
                if half == 1:
                    mm.then_inc(pv_done, 1)

            def steps(step):
                def weigh_part(k, half):
                    if k >= 2 and step.attend:
                        weigh(step, k - 2, 1, half)
                    if k < 2 and step.tail:
                        weigh(step, NCH - 2 + k, 2, half)

                for k in range(NCH):
                    ms = list(M_SLOTS[k]) if step.front else []
                    kv = list(KV_SLOTS[k]) if step.front else []

                    if k == 0 and step.front:
                        pe.wait_ge(c_loaded[step.par], step.half(1) * 16)
                        wait(pe, clow_done, step, 4, 4)
                    if k == 0 and step.i is None and step.u == 1:
                        pe.wait_ge(fills_set, 2)
                        pe.wait_ge(ld_ones, 32)
                    if k == SHIFT_SLOT and step.front:
                        shift_rows(step, 0, 0)
                    for what in PE_FIRST if k == 0 else PE_ORDER:
                        if what == "m" and ms:
                            max_scores(step, ms.pop(0))
                        if what == "K" and kv:
                            project(step, kv.pop(0))
                        if what == "R" and step.attend:
                            shift_rows(step, 1, 1)
                        if what in "01" and step.attend:
                            score_half(step, 2 * k + int(what))
                        if what in "wW":
                            weigh_part(k, "wW".index(what))

            run_steps(pe, steps, B, B + 2)

            def transposes(dst, src, need, done, value):
                pe.wait_ge(ev[need], value)
                for j in range(src.shape[1] // P):
                    mm = nc.tensor.transpose(dst[:, j * P:(j + 1) * P], src[:, j * P:(j + 1) * P], ident)
                mm.then_inc(ev[done], 1)

            def product(dst, lhsT, rhs, done):
                for k in range(KT):
                    mm = nc.tensor.matmul(dst, lhsT[:, k, :], rhs(k), start=(k == 0), stop=(k == KT - 1))
                mm.then_inc(done, 1)

            def product3(dst, n, w, w_low, done, low_event, value):
                for k in range(KT):
                    for part, rhs in enumerate((high(w(k)), w_low(k))):
                        nc.tensor.matmul(dst, rows_high[n][:, k, :], rhs, start=(k == 0 and part == 0), stop=False)
                pe.wait_ge(ev[low_event], value)
                for k in range(KT):
                    mm = nc.tensor.matmul(dst, rows_low[n][:, k, :], high(w(k)), start=False, stop=(k == KT - 1))
                mm.then_inc(done, 1)

            def experts(n, pair, value):
                if pair == 0:
                    pe.wait_ge(ev["h2H"], value)
                cols = slice(2 * pair * D, 2 * (pair + 1) * D)
                product3(bank[n][pair % 2], n, lambda k: we_sb[k][:, cols], lambda k: we_low[k][:, cols], e_ps[pair],
                         "h2L", value)

            pe.wait_ge(ld_t, 16 * 6)
            pe.wait_ge(ld_e, 16)
            pe.wait_ge(ev["out"], 16)
            pe.wait_ge(wqkv_rdy, KT)
            pe.wait_ge(ones_set, 2)
            with pe.Fori(0, TILES // LANES) as group:
                due = values(pe, group)
                y0_due = values(pe, group, LANES)
                for n in lanes:
                    transposes(bank[n][0], rows_in[n], "att_b", "attT_ps", due[n])
                for n in lanes:
                    pe.wait_ge(ev["attT"], due[n])
                    product(bank[n][1][:, 0:D], rows_T[n], lambda k: wo_sb[:, k, :], ev["o_ps"])
                for n in lanes:
                    transposes(bank[n][0], rows_in[n], "h1", "h1T_ps", due[n])
                for n in lanes:
                    pe.wait_ge(ev["h1H"], due[n])
                    for dst, cols, done in ((bank[n][0], slice(0, 2 * D), "qk_ps"),
                                            (bank[n][1][:, 0:D], slice(2 * D, 3 * D), "v_ps")):
                        product3(dst, n, lambda k: wqkv_sb[:, k, cols], lambda k: wqkv_low[:, k, cols], ev[done], "h1L",
                                 due[n])
                for n in lanes:
                    transposes(bank[n][0], rot[n], "rot", "rT_ps", due[n])
                for n in lanes:
                    pe.wait_ge(ev["kbd"], due[n])
                    pe.wait_ge(ev["v"], due[n])
                    for g in range(2):
                        for b in range(2):
                            mm = nc.tensor.matmul(bank[n][g][64 * b:64 * b + 64, :], qkT[n][:, g, 64 * b:64 * b + 64],
                                                  kbd[n][:, g, b, :], start=True, stop=True)
                        mm.then_inc(ev[f"s_ps{g}"], 1)
                for n in lanes:
                    for g in range(2):
                        transposes(bank[n][g], sc[n][:, g, :], "exp", f"pT_ps{g}", due[n])
                for n in lanes:
                    pe.wait_ge(ev["pT"], due[n])
                    for hp in range(HP):
                        for b in range(2):
                            mm = nc.tensor.matmul(bank[n][0][64 * b:64 * b + 64, hp * 32:(hp + 1) * 32],
                                                  pT[n][:, hp, 64 * b:64 * b + 64],
                                                  vbd[n][:, b, hp, :, :].rearrange("p j d -> p (j d)"),
                                                  start=True, stop=True)
                    mm.then_inc(ev["pv_ps"], 1)
                for n in lanes:
                    transposes(bank[n][1], rows_in[n], "att2", "att2T_ps", due[n])
                for n in lanes:
                    pe.wait_ge(ev["att2T"], due[n])
                    product(bank[n][0][:, 0:D], rows_T[n], lambda k: wout_sb[:, k, :], ev["w_ps"])
                for n in lanes:
                    transposes(bank[n][1], rows_in[n], "h2", "h2T_ps", due[n])
                for n in lanes:
                    pe.wait_ge(ev["h2T"], due[n])
                    product(bank[n][0][:, 0:E], rows_T[n], lambda k: wg_sb[:, k, :], ev["lg_ps"])
                pe.wait_ge(we_rdy, 2 * KT)
                for n in lanes:
                    pe.wait_ge(ev["lg"], due[n])
                    experts(n, 0, due[n])
                for n in lanes:
                    pe.wait_ge(ev["mask"], due[n])
                    pe.wait_ge(ev["before"], due[n])
                    nc.tensor.matmul(locations(n), tri, mask[n][:, :], start=True, stop=False)
                    nc.tensor.matmul(locations(n), ones_f[:, :], before[n][:, :], start=False, stop=True)\
                        .then_inc(ev["loc_ps"], 1)
                for n in lanes:
                    pe.wait_ge(ev["wgt"], due[n])
                    nc.tensor.transpose(weights_T(n), wgt[n][:, :], ident).then_inc(ev["wT_ps"], 1)
                for n in lanes:
                    pe.wait_ge(ev["wT"], due[n])
                    nc.tensor.matmul(biases(n), wT[n][:, :], be_sb[:, :], start=True, stop=True).then_inc(ev["b_ps"], 1)
                for pair in range(1, E // 2):
                    for n in lanes:
                        if pair == 1:
                            pe.wait_ge(ev["y0"], y0_due[n])
                        else:
                            pe.wait_ge(y_step[n], added(group, 2 * (pair - 1)))
                        experts(n, pair, due[n])
                for n in lanes:
                    pe.wait_ge(y_step[n], added(group, E))

        @block.scalar
        def _(act):
            for t in range(TILES):
                act.wait_ge(h0T_ps, t + 1)
                for k, hT in enumerate((h0T, h0T2)):
                    cp = nc.scalar.copy(hT[:, t * P:(t + 1) * P], ps_front[:, t % 2, k * P:(k + 1) * P])
                cp.then_inc(h0T_rdy, 1)

            act.wait_ge(qhi_rdy, 1)
            for o in range(KT):
                for j in range(2):
                    cp = nc.scalar.activation(qbd_hi[:, :, o, j * SQ:(j + 1) * SQ],
                                              qhi[o][:, :].rearrange("p (b q) -> p b q", b=B), ACT.Copy,
                                              scale=jmask[:, j:j + 1])
                cp.then_inc(qbd_hi_rdy, 1)

            def high_part(step, u):
                par = step.par
                wait(act, kv_done, step, NKV, KV_POS[u] + 1)
                if u < KUNITS:
                    t, n = divmod(u, NPIECE)
                    n0, nn = piece(n)
                    if n == 0:
                        for r in range(4):
                            wait(act, k_stacked[4 * t + r], step, 48, 0)
                    nc.scalar.activation(khigh[:, t, n0:n0 + nn], kv_bank(step, u)[:, 0:nn], ACT.Identity,
                                         bias=bcol[:, 1, t:t + 1]).then_inc(high_done, 1)
                else:
                    c0 = 2 * (u - KUNITS)
                    nch = min(2, NCH - c0)
                    rows = P if c0 + nch < NCH else LAST
                    if u == KUNITS:
                        wait(act, pv_done, step, NCH, -NCH)
                    nc.scalar.copy(vstack[par][0:rows, c0:c0 + nch, :, 0:32],
                                   kv_bank(step, u)[0:rows, 0:nch * D].rearrange("p (c h d) -> p c h d", c=nch, h=HP))\
                        .then_inc(high_done, 1)

            def exponentials(step, h):
                k, e = divmod(h, 2)
                b = 1 - step.par
                _, nn = keys_of(k)
                slot = P_SLOT[b][k]
                wait(act, score_done, step, 2 * NCH, h + 1 - 2 * NCH)
                if e == 0:
                    wait(act, pv_done, step, NCH, P_PREV[b][k] + 1 - NCH)
                nc.scalar.activation(prob[slot][0:nn, e * 512:e * 512 + 512], ps_score[0:nn, S_BANK[h], :], ACT.Exp)\
                    .then_inc(exp_done, 1)

            def copy_shift(step, half, back):
                wait(act, shift_done, step, 2, half + 1 - 2 * back)
                nc.scalar.copy(qstack[(step.par + back) % 2][96:98, half::2, :],
                               ps_front[96:98, SHIFT_POS[half] % 2, :].rearrange("p (h c) -> p h c", h=4))\
                    .then_inc(shift_copied, 1)

            def steps(step):
                for k in range(NCH):
                    kv = list(KV_SLOTS[k]) if step.front else []
                    if k == SHIFT_SLOT and step.front:
                        copy_shift(step, 0, 0)
                    if k == 2 and step.tail:
                        wait(act, pv_done, step, NCH, -NCH)
                        nc.scalar.copy(osb2[:, :, :], ps_out[:, :, 0:4 * OW]).then_inc(out_copied, 1)
                    for what in ACT_FIRST if k == 0 else ACT_ORDER:
                        if what == "K" and kv:
                            high_part(step, kv.pop(0))
                        if what == "R" and step.attend:
                            copy_shift(step, 1, 1)
                        if what in "01" and step.attend:
                            exponentials(step, 2 * k + int(what))

            run_steps(act, steps, B, B + 2)

            def evacuate(dst, src, need, done, value):
                act.wait_ge(ev[need], value)
                nc.scalar.copy(dst, src).then_inc(ev[done], 1)

            def transposed(src_bank, name, due):
                for n in lanes:
                    evacuate(flat3(rows_T[n]), bank[n][src_bank][:, 0:D], name + "T_ps", name + "T", due[n])
                    if name in ("h1", "h2"):
                        nc.scalar.copy(flat3(rows_high[n]), bank[n][src_bank][:, 0:D]).then_inc(ev[name + "H"], 1)

            with act.Fori(0, TILES // LANES) as group:
                due = values(act, group)
                transposed(0, "att", due)
                transposed(0, "h1", due)
                for n in lanes:
                    evacuate(flat3(qkT[n]), bank[n][0], "rT_ps", "rT", due[n])
                for n in lanes:
                    for g in range(2):
                        act.wait_ge(ev[f"sub{g}"], due[n])
                        e = nc.scalar.activation(sc[n][:, g, :], sc[n][:, g, :], ACT.Exp)
                    e.then_inc(ev["exp"], 1)
                for n in lanes:
                    for g in range(2):
                        act.wait_ge(ev[f"pT_ps{g}"], due[n])
                        cp = nc.scalar.copy(flat3(pT[n])[:, g * 512:(g + 1) * 512], bank[n][g])
                    cp.then_inc(ev["pT"], 1)
                transposed(1, "att2", due)
                transposed(1, "h2", due)
                for n in lanes:
                    act.wait_ge(ev["lneg"], due[n])
                    nc.scalar.activation(ex[n][:, :], lg[n][:, :], ACT.Exp, bias=lneg[n][:, :], accum_out=lsum[n][:, :])\
                        .then_inc(ev["ex"], 1)
                for n in lanes:
                    evacuate(wT[n][:, :], weights_T(n), "wT_ps", "wT", due[n])

        @block.vector
        def _(dve):
            count = [0]

            def link(ins):
                count[0] += 1
                ins.then_inc(chain0, 1)
                dve.wait_ge(chain0, count[0])

            for p in range(2):
                nc.vector.memset(vstack[p][:, :, :, 64:66], 1.0).then_inc(fills_set, 1)
            dve.wait_ge(ld_x, 16)
            for t in range(TILES):
                st = nc.vector.bn_stats(st0[:, t, :], x_all[:, t * D:(t + 1) * D])
            link(st)
            for t in range(TILES):
                ag = nc.vector.bn_aggr(mv0[:, t, :], st0[:, t, :])
            link(ag)
            nc.vector.tensor_scalar_add(ve0[:, :], mv0[:, :, 1], EPS).then_inc(ve0_rdy, 1)
            dve.wait_ge(ld_b, 16)
            nc.vector.tensor_scalar_mul(bq4[:, :], bcol[:, 0, :], DH ** -0.5)
            dve.wait_ge(ld_c, 16)
            nc.vector.tensor_copy(ident_bf[:, :], ident)
            dve.wait_ge(rs0_rdy, 1)
            for t in range(TILES):
                if t >= 4:
                    dve.wait_ge(h0T_ps, t - 3)
                nc.vector.tensor_scalar(h0[:, t % 4, :], x_all[:, t * D:(t + 1) * D], mv0[:, t, 0:1], rs0[:, t:t + 1],
                                        ALU.subtract, ALU.mult).then_inc(h0_rdy, 1)
            dve.wait_ge(ld_w, 32)
            for n in range(2):
                nc.vector.tensor_copy(w_hi[n][:, :, :], w_f[n][:, :, :]).then_inc(w_rdy, 1)
            dve.wait_ge(w_rdy, 2)
            for n in range(2):
                nc.vector.tensor_tensor(w_lo[n][:, :, :], w_f[n][:, :, :], w_hi[n][:, :, :], ALU.subtract)\
                    .then_inc(w_rdy, 1)
            for o in range(KT):
                for half in range(2):
                    dve.wait_ge(q_ps, 2 * o + half + 1)
                    last = nc.vector.tensor_scalar(
                        qT[o][:, half * 512:half * 512 + 512], ps_score[:, half, :] if o == 0 else ps_out[:, half, :],
                        DH ** -0.5, bq4[:, o:o + 1], ALU.mult, ALU.add)
            link(last)
            for o in range(KT):
                last = nc.vector.tensor_copy(qhi[o][:, :], qT[o][:, :])
            last.then_inc(qhi_rdy, 1)
            dve.wait_ge(qhi_rdy, 1)
            for o in range(KT):
                last = nc.vector.tensor_tensor(qlo[o][:, :], qT[o][:, :], qhi[o][:, :], ALU.subtract)
            link(last)
            for o in range(KT):
                for j in range(2):
                    last = nc.vector.tensor_scalar(qbd_lo[:, :, o, j * SQ:(j + 1) * SQ],
                                                   qlo[o][:, :].rearrange("p (b q) -> p b q", b=B), jmask[:, j:j + 1], None,
                                                   ALU.mult)
                last.then_inc(qbd_rdy, 1)
            nc.vector.memset(before[0][:, :], 0.0).then_inc(ev["before"], 1)

            def low_prob(step, k):
                b = 1 - step.par
                _, nn = keys_of(k)
                slot = P_SLOT[b][k]
                wait(dve, exp_done, step, 2 * NCH, 2 * k + 2 - 2 * NCH)
                wait(dve, pv_done, step, NCH, P_PREV[b][k] + 1 - NCH)
                nc.vector.tensor_tensor(plow[slot][0:nn, :], prob[slot][0:nn, :], p_high(slot, 0, HP * P)[0:nn],
                                        ALU.subtract).then_inc(plow_dve, 1)

            def low_part(step, u):
                par = step.par
                wait(dve, high_done, step, NKV, KV_POS[u] + 1)
                if u < KUNITS:
                    t, n = divmod(u, NPIECE)
                    n0, nn = piece(n)
                    if n == 0:
                        for r in range(4):
                            wait(dve, k_stacked[4 * t + r], step, 48, 0)
                    nc.vector.scalar_tensor_tensor(klow[:, t, n0:n0 + nn], kv_bank(step, u)[:, 0:nn], bcol[:, 1, t:t + 1],
                                                   khigh[:, t, n0:n0 + nn], ALU.add, ALU.subtract).then_inc(kv_free, 1)
                else:
                    c0 = 2 * (u - KUNITS)
                    nch = min(2, NCH - c0)
                    rows = P if c0 + nch < NCH else LAST
                    v = vstack[par][0:rows, c0:c0 + nch, :, :]
                    nc.vector.tensor_tensor(v[:, :, :, 32:64],
                                            kv_bank(step, u)[0:rows, 0:nch * D].rearrange("p (c h d) -> p c h d", c=nch, h=HP),
                                            v[:, :, :, 0:32], ALU.subtract).then_inc(kv_free, 1)

            def maximum(step, m):
                wait(dve, m_done, step, MUNITS, m + 1)
                ps = ps_front[:, front_pos(m) % 2, :]
                unit = max_unit(m)
                _, hp, n = unit[0]
                _, nn = piece(n)
                nc.vector.reduce_max(maxes[:, hp:hp + len(unit), n],
                                     ps[:, 0:len(unit) * nn].rearrange("p (h k) -> p h k", k=nn), AX.X).then_inc(m_free, 1)
                if m % (MUNITS // 2) == MUNITS // 2 - 1:
                    shift(step, m // (MUNITS // 2))

            def shift(step, half):
                hps = slice(4 * half, 4 * half + 4)
                wait(dve, m_free, step, MUNITS, (half + 1) * (MUNITS // 2))
                if half == 0:
                    wait(dve, shift_done, step, 2, 0)
                nc.vector.tensor_reduce(negmax[:, hps], maxes[:, hps, :], AX.X, ALU.max, negate=True).then_inc(max_done, 1)
                wait(dve, max_done, step, 4, 2 * half + 1)
                nc.vector.tensor_copy(mparts[:, hps, 0], negmax[:, hps]).then_inc(max_done, 1)
                wait(dve, max_done, step, 4, 2 * half + 2)
                nc.vector.tensor_tensor(mparts[:, hps, 1], negmax[:, hps], mparts[:, hps, 0], ALU.subtract)\
                    .then_inc(shift_ready, 1)

            def attended(step):
                wait(dve, out_copied, step, 1, -1)
                nc.vector.reciprocal(orec[:, :], osb[:, :, 64])
                nc.vector.tensor_tensor(osum[:, :, :], osb[:, :, 0:32], osb[:, :, 32:64], ALU.add).then_inc(out_summed, 1)
                wait(dve, out_summed, step, 1, -1)
                col = step.half(-1) * D
                rows = slice(64 * step.par, 64 * step.par + 64)
                for j in range(2):
                    half = slice(64 * j, 64 * j + 64)
                    dst = att_all[rows, bass.ds(col, D)] if step.i is not None else att_all[rows, col:col + D]
                    nc.vector.tensor_tensor(dst.rearrange("p (h j d) -> p h j d", h=HP, j=2)[:, :, j, :],
                                            osum[half, :, j * DH:(j + 1) * DH],
                                            orec[half, :].unsqueeze(2).to_broadcast([64, HP, DH]), ALU.mult)\
                        .then_inc(att_done, 1)

            def steps(step):
                for k in range(NCH):
                    ms = list(M_SLOTS[k]) if step.front else []
                    kv = list(KV_SLOTS[k]) if step.front else []
                    for what in DVE_FIRST if k == 0 else DVE_ORDER:
                        if what == "m" and ms:
                            maximum(step, ms.pop(0))
                        if what == "K" and kv:
                            low_part(step, kv.pop(0))
                        if what == "p" and step.attend and k >= 1 and k - 1 in low_chunks(step, 1)[1]:
                            low_prob(step, k - 1)
                        if what == "a" and k == 3 and step.tail:
                            attended(step)

            run_steps(dve, steps, B, B + 2)

            def tt(out_, a, b, op, done, value, need=()):
                for name in need:
                    dve.wait_ge(ev[name], value)
                nc.vector.tensor_tensor(out_, a, b, op).then_inc(ev[done], 1)

            def moments(n, a, src_ev, due):
                dve.wait_ge(ev[src_ev], due[n])
                nc.vector.bn_stats(stats[n][:, :], x_a[n]).then_inc(ev["stats" + a], 1)
                dve.wait_ge(ev["stats" + a], due[n])
                nc.vector.tensor_copy(spare[n][:, :], x_a[n][:, 0:1])
                nc.vector.bn_aggr(mv[n][:, :], stats[n][:, :]).then_inc(ev["agg" + a], 1)
                dve.wait_ge(ev["agg" + a], due[n])
                nc.vector.tensor_scalar_add(ve[n][:, :], mv[n][:, 1:2], EPS).then_inc(ev["var" + a], 1)

            def normalised(n, a, due):
                dve.wait_ge(ev["rs" + a], due[n])
                nc.vector.tensor_scalar(rows_in[n], x_a[n], mv[n][:, 0:1], rs[n][:, :], ALU.subtract, ALU.mult)\
                    .then_inc(ev["h" + a], 1)

            heads = lambda a: a.rearrange("p (h d) -> p h d", d=DH)
            by_key = lambda a: a.rearrange("p (h k) -> p h k", h=8)

            dve.wait_ge(ld_t, 16 * 6)
            dve.wait_ge(att_done, 2 * B)
            for n in lanes:
                nc.vector.memset(vbd[n][:, :, :, :, :], 0.0).then_inc(ev["y0"], 1)
            dve.wait_ge(ev["y0"], LANES)
            with dve.Fori(0, TILES // LANES) as group:
                due = values(dve, group)
                y0_due = values(dve, group, LANES)
                for n in lanes:
                    tt(x_a[n], bank[n][1][:, 0:D], x_a[n], ALU.add, "x1", due[n], ("xb", "o_ps"))
                    moments(n, "1", "x1", due)
                    if n:
                        normalised(n - 1, "1", due)
                normalised(LANES - 1, "1", due)
                for n in lanes:
                    tt(qk[n], bank[n][0], brow[:, 2:4, :].rearrange("p a n -> p (a n)"), ALU.add, "qk", due[n], ("qk_ps",))
                    qh, rh = heads(qk[n]), heads(rot[n])
                    tt(rh[:, :, 0:8], qh[:, :, 0:8], qh[:, :, 1:DH:2], ALU.subtract, "rotA", due[n], ("qk",))
                    tt(rh[:, :, 8:DH], qh[:, :, 8:DH], qh[:, :, 0:DH:2], ALU.add, "rotB", due[n])
                    dve.wait_ge(ev["rotA"], due[n])
                    dve.wait_ge(ev["rotB"], due[n])
                    for a in range(2):
                        part = heads(rot[n][:, a * D:(a + 1) * D])
                        tab = rope[:, a * DH:(a + 1) * DH].unsqueeze(1).to_broadcast([P, HEADS, DH])
                        last = nc.vector.tensor_tensor(part, part, tab, ALU.mult)
                    last.then_inc(ev["rot"], 1)
                    dve.wait_ge(ev["v_ps"], due[n])
                    for b in range(2):
                        rows = slice(64 * b, 64 * b + 64)
                        for j in range(2):
                            vin = bank[n][1][rows, 0:D].rearrange("p (h j d) -> p h j d", h=HP, j=2)[:, :, j, :]
                            bin_ = brow[rows, 4, :].rearrange("p (h j d) -> p h j d", h=HP, j=2)[:, :, j, :]
                            last = nc.vector.tensor_tensor(vbd[n][64 * j:64 * j + 64, b, :, j, :], vin, bin_, ALU.add)
                    last.then_inc(ev["v"], 1)
                for n in lanes:
                    dve.wait_ge(ev["rT"], due[n])
                    for g in range(2):
                        for b in range(2):
                            last = nc.vector.tensor_tensor(
                                by_key(kbd[n][:, g, b, :]),
                                qkT[n][:, 2 + g, 64 * b:64 * b + 64].unsqueeze(1).to_broadcast([P, 8, SQ]),
                                mask8.unsqueeze(2).to_broadcast([P, 8, SQ]), ALU.mult)
                    last.then_inc(ev["kbd"], 1)
                for n in lanes:
                    for g in range(2):
                        dve.wait_ge(ev[f"s_ps{g}"], due[n])
                        nc.vector.reduce_max(smax[n][:, 8 * g:8 * g + 8], by_key(bank[n][g]), AX.X)\
                            .then_inc(ev[f"smax{g}"], 1)
                    for g in range(2):
                        tt(by_key(sc[n][:, g, :]), by_key(bank[n][g]),
                           smax[n][:, 8 * g:8 * g + 8].unsqueeze(2).to_broadcast([P, 8, SQ]), ALU.subtract, f"sub{g}",
                           due[n], (f"smax{g}",))
                for n in lanes:
                    dve.wait_ge(ev["exp"], due[n])
                    nc.vector.reduce_sum(ssum[n][:, :], sc[n].rearrange("p g (h k) -> p (g h) k", h=8), AX.X)\
                        .then_inc(ev["ssum"], 1)
                for n in lanes:
                    dve.wait_ge(ev["ssum"], due[n])
                    nc.vector.reciprocal(srec[n][:, :], ssum[n][:, :]).then_inc(ev["srec"], 1)
                for n in lanes:
                    tt(heads(rows_in[n]), heads(bank[n][0][:, 0:D]), srec[n][:, :].unsqueeze(2).to_broadcast([P, HEADS, DH]),
                       ALU.mult, "att2", due[n], ("srec", "pv_ps"))
                for n in lanes:
                    tt(x_a[n], bank[n][0][:, 0:D], x_b[n], ALU.add, "x2", due[n], ("x_b", "w_ps"))
                    moments(n, "2", "x2", due)
                    if n:
                        normalised(n - 1, "2", due)
                normalised(LANES - 1, "2", due)
                for n in lanes:
                    dve.wait_ge(ev["lg_ps"], due[n])
                    nc.vector.tensor_copy(lg[n][:, :], bank[n][0][:, 0:E]).then_inc(ev["lg"], 1)
                for n in lanes:
                    dve.wait_ge(ev["lg"], due[n])
                    nc.vector.reduce_max(lmax[n][:, :], lg[n][:, :], AX.X).then_inc(ev["lmax"], 1)
                for n in lanes:
                    dve.wait_ge(ev["lmax"], due[n])
                    nc.vector.tensor_scalar_mul(lneg[n][:, :], lmax[n][:, :], -1.0).then_inc(ev["lneg"], 1)
                    nc.vector.scalar_tensor_tensor(eq[n][:, :], lg[n][:, :], lmax[n][:, :], desc, ALU.is_equal, ALU.mult)\
                        .then_inc(ev["ranked"], 1)
                for n in lanes:
                    dve.wait_ge(ev["ranked"], due[n])
                    nc.vector.reduce_max(first[n][:, :], eq[n][:, :], AX.X).then_inc(ev["first"], 1)
                for n in lanes:
                    dve.wait_ge(ev["first"], due[n])
                    nc.vector.tensor_scalar(mask[n][:, :], desc, first[n][:, :], None, ALU.is_equal).then_inc(ev["mask"], 1)
                for n in lanes:
                    if n == LANES - 1:
                        dve.wait_ge(ev["loc_ps"], due[0])
                    tt(before[(n + 1) % LANES][:, :], before[n][:, :], mask[n][:, :], ALU.add, "before", due[n],
                       ("mask", "before"))
                for n in lanes:
                    dve.wait_ge(ev["ex"], due[n])
                    nc.vector.reciprocal(gate[n][:, :], lsum[n][:, :]).then_inc(ev["gate"], 1)
                for n in lanes:
                    dve.wait_ge(ev["loc_ps"], due[n])
                    nc.vector.scalar_tensor_tensor(keep[n][:, :], locations(n), float(CAP), mask[n][:, :], ALU.is_lt,
                                                   ALU.mult).then_inc(ev["keep"], 1)
                for n in lanes:
                    dve.wait_ge(ev["keep"], due[n])
                    dve.wait_ge(ev["gate"], due[n])
                    nc.vector.tensor_scalar(wgt[n][:, :], keep[n][:, :], gate[n][:, :], None, ALU.mult)\
                        .then_inc(ev["wgt"], 1)
                for n in lanes:
                    tt(x_b[n], biases(n), x_a[n], ALU.add, "y0", due[n], ("b_ps",))
                for e in range(E):
                    for n in lanes:
                        if e % 2 == 0:
                            dve.wait_ge(e_ps[e // 2], due[n])
                        if e == 0:
                            dve.wait_ge(ev["y0"], y0_due[n])
                        else:
                            dve.wait_ge(y_step[n], added(group, e))
                        nc.vector.scalar_tensor_tensor(x_b[n], bank[n][e // 2 % 2][:, (e % 2) * D:(e % 2 + 1) * D],
                                                       wgt[n][:, e:e + 1], x_b[n], ALU.mult, ALU.add)\
                            .then_inc(y_step[n], 1)
                for n in lanes:
                    dve.wait_ge(y_step[n], added(group, E))
                    nc.vector.tensor_copy(spare[n][:, :], x_b[n][:, 0:1]).then_inc(ev["y"], 1)


_INS = ["x", "ctxT", "wqT", "wkT", "wvT", "bqk", "woT", "wqkv", "wout", "brows", "wg", "weT", "be", "consts", "ones2"]


def shape_constants():
    c = np.zeros((P, NCONST), np.float32)
    p = np.arange(P)
    c[:, C_ID:C_ID + P] = np.eye(P)
    c[:, C_TRI:C_TRI + P] = p[:, None] < p[None, :]
    c[:, C_MASK:C_MASK + 8] = (p[:, None] // DH) == np.arange(8)[None, :]
    c[:, C_J:C_J + 2] = (p[:, None] // DH % 2) == np.arange(2)[None, :]
    c[:, C_DESC:C_DESC + E] = E - np.arange(E)
    theta = np.float32(10000.0) ** (-np.arange(0, DH, 2, dtype=np.float32) / np.float32(DH))
    freqs = (p % SQ).astype(np.float32)[:, None] * theta[None, :]
    table = np.concatenate([np.sin(freqs), np.cos(freqs)], axis=-1).astype(np.float32)
    c[:, C_ROPE:C_ROPE + DH] = table * np.float32(DH ** -0.5)
    c[:, C_ROPE + DH:] = table
    return c


def kernel(**inputs):
    import numpy as _np
    import concourse.bacc as _bacc
    from concourse import mybir as _mybir
    from concourse.bass_utils import run_bass_kernel_spmd as _run

    a = {k: _np.asarray(v) for k, v in inputs.items()}
    t = lambda v, *axes: _np.ascontiguousarray(_np.transpose(v, axes))
    arrays = {
        "x": a["x"].reshape(B * SQ, D), "ctxT": t(a["ctx_1024"], 0, 2, 1),
        "wqT": t(a["L0_xattn_Wq"], 1, 0),
        "wkT": t(a["L0_xattn_Wk"], 1, 0),
        "wvT": t(a["L0_xattn_Wv"], 1, 0),
        "woT": t(a["L0_xattn_Wo"], 1, 0),
        "wqkv": a["L0_attn_Wqkv"], "wout": a["L0_attn_Wout"],
        "wg": a["L0_ffn_wg"], "weT": t(a["L0_ffn_W"], 0, 2, 1), "be": a["L0_ffn_b"], "consts": shape_constants(),
        "ones2": np.full((2, HP * SKP // 2), ONES2, np.float32),
        "bqk": t(_np.stack([a["L0_xattn_bq"], a["L0_xattn_bk"]]).reshape(2, KT, P), 2, 0, 1),
        "brows": _np.concatenate([a["L0_xattn_bv"], a["L0_xattn_bo"], a["L0_attn_bqkv"], a["L0_attn_bout"]]),
    }
    nc = _bacc.Bacc("TRN2", target_bir_lowering=False, num_devices=1)
    args, ins = [], {}
    for name in _INS:
        v = _np.ascontiguousarray(arrays[name])
        ins[f"in_{name}"] = v
        args.append(nc.dram_tensor(f"in_{name}", v.shape, _mybir.dt.from_np(v.dtype), kind="ExternalInput").ap())
    args.append(nc.dram_tensor("out_0", (B * SQ, D), _mybir.dt.float32, kind="ExternalOutput").ap())
    build(nc, *args)
    r = _run(nc, [ins], core_ids=[0])
    return r.results[0]["out_0"].reshape(B, SQ, D)
```

```python
import numpy as np
import concourse.bass as bass
from concourse import mybir
from contextlib import ExitStack

P = 128
D = 256
KT = D // P
HEADS = 16
DH = D // HEADS
B = 16
SQ = 64
SK = 1601
NCH = -(-SK // P)
SKP = SK + SK % 2
LAST = SK - (NCH - 1) * P
HP = HEADS // 2
TILES = B * SQ // P
E = 8
CAP = B * SQ // E
EPS = 1e-5
VW = 66
OW = 65
NPAR = 4
NSB = 2
QSENT = 16 * 3 * 4
LANES = 2
ROUNDS = TILES // LANES

C_ID, C_TRI, C_MASK, C_J, C_DESC, C_ROPE = 0, 128, 256, 264, 266, 274
NCONST = C_ROPE + 2 * DH

NPIECE = -(-SK // 512)
KUNITS = KT * NPIECE
VUNITS = -(-NCH // 2)
NKV = KUNITS + VUNITS
FULL = SK // 512
MUNITS = 2 * (4 * FULL + 1)
NM = MUNITS + 2
KV_SLOTS = [[0, 1], [2, 3], [8, 9], [4, 5], [6], [10, 7], [], [11], [12], [13], [], [], [14]]
M_COUNT = [0, 0, 0, 3, 1, 2, 2, 4, 4, 3, 2, 2, 3]
M_SLOTS = [list(range(sum(M_COUNT[:k]), sum(M_COUNT[:k + 1]))) for k in range(NCH)]
PE_ORDER, PE_FIRST = '0mKm1mwWKm', 'K0RmmKm1wKWm'
DVE_ORDER, DVE_FIRST = 'mpammKmK', 'KmapmKKmm'
ACT_ORDER, ACT_FIRST = '0K1K', 'KR0K1K'
LOW_AT = [0, 0, 0, 4]
SHIFT_SLOT = 10
SHIFT_POS = [M_SLOTS[SHIFT_SLOT][0], NM - 1]


def max_unit(m):
    half, nth = divmod(m, 4 * FULL + 1)
    if nth < 4 * FULL:
        return [(0, 4 * half + nth // FULL, nth % FULL)]
    rest = SK - FULL * 512
    return [(j * rest, 4 * half + j, FULL) for j in range(4)]


def q_at(hp):
    return 2 * (hp % 4) + hp // 4


def front_pos(m):
    return m + (m >= SHIFT_POS[0])


KV_POS = {u: n for n, u in enumerate(u for slot in KV_SLOTS for u in slot)}
GPS_CHUNKS = [2, 4, 5, 6, 7, 8, 9, 10, 11, 12]
DVE_CHUNKS = [k for k in range(NCH) if k not in GPS_CHUNKS]
LAST_GPS = [0, 3, 6, 9]
LAST_DVE = [k for k in range(NCH) if k not in LAST_GPS]


def piece(n):
    return n * 512, min(512, SK - n * 512)


def keys_of(k):
    return k * P, (P if k < NCH - 1 else LAST)


ONES2 = float(np.array([0x3F803F80], np.uint32).view(np.float32)[0])


class Step:

    def __init__(self, i, u):
        self.i, self.u, self.par = i, u, u % 2
        self.front = i is not None or u < B
        self.attend = i is not None or 1 <= u <= B
        self.tail = i is not None or u >= 2

    def at(self, n, c):
        return n * self.u + c if self.i is None else self.i * (2 * n) + (n * self.u + c)

    def half(self, c):
        return self.u // 2 + c if self.i is None else self.i + (self.u // 2 + c)


def low_chunks(step, back):
    last = step.i is None and step.u - back == B - 1
    return (LAST_GPS, LAST_DVE) if last else (GPS_CHUNKS, DVE_CHUNKS)


def wait(eng, sem, step, n, c):
    if step.i is None and n * step.u + c <= 0:
        return
    assert n * step.u + c > 0
    eng.wait_ge(sem, step.at(n, c))


def run_steps(eng, emit, upto, last):
    emit(Step(None, 0))
    emit(Step(None, 1))
    with eng.Fori(0, (upto - 2) // 2) as i:
        emit(Step(i, 2))
        emit(Step(i, 3))
    for u in range(upto, last):
        emit(Step(None, u))


def last_use(k, slots_now, slots_before):
    for j in range(k - 1, -1, -1):
        if slots_now[j] == slots_now[k]:
            return j
    n = len(slots_before)
    for j in range(n - 1, -1, -1):
        if slots_before[j] == slots_now[k]:
            return j - n
    raise ValueError(k)


S_BANK = [h % NSB for h in range(2 * NCH)]
P_SLOT = [[(k + par) % NPAR for k in range(NCH)] for par in range(2)]
S_PREV = [last_use(h, S_BANK, S_BANK) for h in range(2 * NCH)]
P_PREV = [[last_use(k, P_SLOT[par], P_SLOT[1 - par]) for k in range(NCH)] for par in range(2)]


def build(nc, x, ctxT, wqT, wkT, wvT, bqk, woT, wqkv, wout, brows, wg, weT, be, consts, ones2, out):
    f32, bf16 = mybir.dt.float32, mybir.dt.bfloat16
    ALU, ACT, AX = mybir.AluOpType, mybir.ActivationFunctionType, mybir.AxisListType
    ctx = ExitStack()
    with ctx:
        def sb(name, shape, dt=f32):
            return ctx.enter_context(nc.sbuf_tensor(name, shape, dt))

        def sem(name):
            return ctx.enter_context(nc.semaphore(name))

        cst = sb("cst", [P, NCONST])
        ident, tri = cst[:, C_ID:C_ID + P], cst[:, C_TRI:C_TRI + P]
        mask8, jmask = cst[:, C_MASK:C_MASK + 8], cst[:, C_J:C_J + 2]
        desc, rope = cst[:, C_DESC:C_DESC + E], cst[:, C_ROPE:C_ROPE + 2 * DH]
        ident_bf = sb("ident_bf", [P, P], bf16)
        ones_f = sb("ones_f", [P, P])
        half_neg = sb("half_neg", [P, TILES])
        x_all = sb("x_all", [P, TILES * D])
        att_all = sb("att_all", [P, TILES * D])
        cbuf = [sb(f"cbuf{p}", [P, KT, SK]) for p in range(2)]
        clow = [sb(f"clow{p}", [P, KT, SK], bf16) for p in range(2)]
        khigh = sb("khigh", [P, KT, SKP], bf16)
        klow = sb("klow", [P, KT, SKP], bf16)
        kstack = [sb(f"kstack{p}", [P, HP, SKP], bf16) for p in range(2)]
        vstack = [sb(f"vstack{p}", [P, NCH, HP, VW], bf16) for p in range(2)]
        qstack = [sb(f"qstack{p}", [P, HP, P], bf16) for p in range(2)]
        prob = [sb(f"prob{p}", [P, HP * P]) for p in range(NPAR)]
        plow = [sb(f"plow{p}", [P, HP * P], bf16) for p in range(NPAR)]
        maxes = sb("maxes", [P, HP, NPIECE])
        negmax = sb("negmax", [P, HP])
        mparts = sb("mparts", [P, HP, 2], bf16)
        osb2 = sb("osb", [P, 2, 4 * OW])
        osb = osb2[:, :, :].rearrange("p a (h c) -> p (a h) c", c=OW)
        osum = sb("osum", [P, HP, 2 * DH])
        orec = sb("orec", [P, HP])
        w_f = [att_all[:, n * KT * D:(n + 1) * KT * D].rearrange("p (k n) -> p k n", k=KT) for n in range(2)]
        w_hi = [sb(f"w_hi{n}", [P, KT, D], bf16) for n in range(2)]
        w_lo = [sb(f"w_lo{n}", [P, KT, D], bf16) for n in range(2)]
        bcol = sb("bcol", [P, 2, KT])
        bq4 = sb("bq4", [P, KT])

        wq_sb = prob[0][:, 0:KT * D].rearrange("p (k n) -> p k n", k=KT)
        h0 = prob[1][:, :].rearrange("p (t n) -> p t n", n=D)
        h0T = [cbuf[1][:, k, 0:B * SQ] for k in range(KT)]
        qT = [prob[2], prob[3]]
        qhi = [plow[0], plow[1]]
        qlo = [plow[2], plow[3]]
        qbd_hi = kstack[1][:, 0:4, :].rearrange("p a n -> p (a n)")[:, 0:B * 2 * P]\
            .rearrange("p (b t c) -> p b t c", b=B, t=KT)
        qbd_lo = kstack[1][:, 4:8, :].rearrange("p a n -> p (a n)")[:, 0:B * 2 * P]\
            .rearrange("p (b t c) -> p b t c", b=B, t=KT)
        q_dram = nc.dram_tensor("q_stacked", [B, 96, HP, P], bf16, kind="Internal").ap()
        st0 = sb("st0", [P, TILES, 6])
        mv0 = sb("mv0", [P, TILES, 2])
        ve0 = sb("ve0", [P, TILES])
        rs0 = sb("rs0", [P, TILES])

        wo_sb = sb("wo_sb", [P, KT, D])
        wqkv_sb = sb("wqkv_sb", [P, KT, 3 * D])
        wqkv_low = sb("wqkv_low", [P, KT, 3 * D], bf16)
        wout_sb = sb("wout_sb", [P, KT, D])
        wg_sb = sb("wg_sb", [P, KT, E])
        be_sb = sb("be_sb", [E, D])
        brow = sb("brow", [P, 6, D])
        we_sb = [cbuf[k][:, :, :].rearrange("p k n -> p (k n)")[:, 0:E * D] for k in range(KT)]
        flat3 = lambda a: a[:, :, :].rearrange("p a b -> p (a b)")
        we_low = [flat3(clow[k])[:, 0:E * D] for k in range(KT)]
        rooms = [flat3(kstack[p]).bitcast(f32) for p in range(2)]
        rooms += [vstack[p][:, :, :, :].rearrange("p c h n -> p (c h n)").bitcast(f32) for p in range(2)]
        rooms += [prob[p][:, :] for p in range(NPAR)] + [flat3(a).bitcast(f32) for a in (khigh, klow)]
        used = [0] * len(rooms)

        def carve(n):
            r = min(r for r in range(len(rooms)) if used[r] + n <= rooms[r].shape[1])
            used[r] += n
            return rooms[r][:, used[r] - n:used[r]]

        lanes = range(LANES)
        kbd_flat = [carve(4 * 512) for _ in lanes]
        kbd = [a.rearrange("p (g b n) -> p g b n", g=2, b=2) for a in kbd_flat]
        pT = [a[:, 0:HP * P].rearrange("p (h n) -> p h n", h=HP) for a in kbd_flat]
        sc = [carve(2 * 512).rearrange("p (g n) -> p g n", g=2) for _ in lanes]
        qk, rot = [carve(2 * D) for _ in lanes], [carve(2 * D) for _ in lanes]
        qkT = [carve(2 * D).rearrange("p (k n) -> p k n", k=4) for _ in lanes]
        vbd = [carve(2 * D).rearrange("p (b h j d) -> p b h j d", b=2, h=HP, j=2) for _ in lanes]
        f_rows, f_x = [carve(D) for _ in lanes], [carve(D) for _ in lanes]
        b_rows, b_res, b_x, b_y = ([carve(D) for _ in lanes] for _ in range(4))
        f_T, b_T = ([carve(D).rearrange("p (k n) -> p k n", k=KT) for _ in lanes] for _ in range(2))
        f_high, f_low, b_high, b_low = ([carve(D // 2).bitcast(bf16).rearrange("p (k n) -> p k n", k=KT) for _ in lanes]
                                        for _ in range(4))

        def lane_tiles(name, shape):
            return [sb(f"{name}_{n}", shape) for n in lanes]

        smax, ssum, srec = (lane_tiles(n, [P, HEADS]) for n in ("smax", "ssum", "srec"))
        stats, mv, ve, rs = ({a: lane_tiles(n + a, shape) for a in "12"} for n, shape in
                             (("stats", [P, 6]), ("mv", [P, 2]), ("ve", [P, 1]), ("rs", [P, 1])))
        lg, ex, eq, mask, keep, wgt = (lane_tiles(n, [P, E]) for n in ("lg", "ex", "eq", "mask", "keep", "wgt"))
        before = lane_tiles("before", [P, E])
        lmax, lneg, lsum, first, gate, spare = (lane_tiles(n, [P, 1]) for n in
                                                ("lmax", "lneg", "lsum", "first", "gate", "spare"))
        wT = lane_tiles("wT", [E, P])

        ps_kv = ctx.enter_context(nc.psum_tensor("ps_kv", [P, 2, 512], f32))
        ps_front = ctx.enter_context(nc.psum_tensor("ps_front", [P, 2, 512], f32))
        ps_score = ctx.enter_context(nc.psum_tensor("ps_score", [P, NSB, 512], f32))
        ps_out = ctx.enter_context(nc.psum_tensor("ps_out", [P, 2, 512], f32))
        f_bank = [[pair[:, n, :] for n in range(2)] for pair in (ps_kv, ps_front)]
        b_bank = [[pair[:, n, :] for n in range(2)] for pair in (ps_score, ps_out)]

        ld_ones, qhi_rdy, qbd_hi_rdy = sem("ld_ones"), sem("qhi_rdy"), sem("qbd_hi_rdy")
        ld_x, ld_c, ld_w, ld_wq, ld_b, ld_t, ld_e = (
            sem(n) for n in ("ld_x", "ld_c", "ld_w", "ld_wq", "ld_b", "ld_t", "ld_e"))
        ones_set, chain0, ve0_rdy, rs0_rdy = (sem(n) for n in ("ones_set", "chain0", "ve0_rdy", "rs0_rdy"))
        fills_set = sem("fills_set")
        h0_rdy, h0T_ps, h0T_rdy, q_ps, qbd_lo_rdy, q_sent, w_rdy = (
            sem(n) for n in ("h0_rdy", "h0T_ps", "h0T_rdy", "q_ps", "qbd_lo_rdy", "q_sent", "w_rdy"))
        c_loaded = [sem("c_loaded0"), sem("c_loaded1")]
        q_loaded = sem("q_loaded")
        k_stacked = [sem(f"k_stacked{hp}") for hp in range(HP)]
        clow_done = sem("clow_done")
        kv_done, kv_free, high_done = sem("kv_done"), sem("kv_free"), sem("high_done")
        m_done, m_free = sem("m_done"), sem("m_free")
        max_done, shift_ready, shift_done, shift_copied = (
            sem(n) for n in ("max_done", "shift_ready", "shift_done", "shift_copied"))
        score_done, exp_done, pv_done = sem("score_done"), sem("exp_done"), sem("pv_done")
        plow_dve, plow_gps = sem("plow_dve"), sem("plow_gps")
        out_copied, out_summed, att_done = sem("out_copied"), sem("out_summed"), sem("att_done")

        ev = {n: sem("t_" + n) for n in (
            "att_b", "attT_ps", "attT", "o_ps", "xb", "x1", "stats1", "agg1", "var1", "rs1", "res",
            "h1", "h1T_ps", "h1T", "h1H", "h1L", "qk_ps", "qk", "v_ps", "v", "rotA", "rotB", "rot",
            "rT_ps", "rT", "kbd", "s_ps0", "s_ps1", "smax0", "smax1", "sub0", "sub1", "exp",
            "ssum", "srec", "pT_ps0", "pT_ps1", "pT", "pv_ps", "att2", "att2T_ps", "att2T",
            "w_ps", "x2", "stats2", "agg2", "var2", "rs2", "h2", "h2T_ps", "h2T", "h2H", "h2L",
            "lg_ps", "lg", "lmax", "lneg", "ranked", "first", "mask", "ex", "gate", "loc_ps",
            "keep", "before", "wgt", "wT_ps", "wT", "b_ps", "y0", "y", "out")}
        e_ps = [sem(f"t_e_ps{n}") for n in range(E // 2)]
        wqkv_rdy, we_rdy = sem("t_wqkv_rdy"), sem("t_we_rdy")
        vbd_zero = sem("t_vbd_zero")
        y_step = [sem(f"t_y_step{n}") for n in lanes]

        locations = lambda n: b_bank[n][1][:, 0:E]
        weights_T = lambda n: b_bank[n][1][0:E, P:2 * P]
        biases = lambda n: b_bank[n][1][:, D:2 * D]

        def added(p, n):
            return p * E + n

        def values(eng, p, back=0):
            due = [p * LANES + (n + 1 - back * LANES) for n in lanes]
            return due if isinstance(p, int) else [eng.snap(value) for value in due]

        def rounds(eng, emit):
            emit(0, values(eng, 0), None)
            with eng.Fori(1, ROUNDS) as p:
                emit(p, values(eng, p), values(eng, p, 1))
            emit(ROUNDS, None, values(eng, ROUNDS, 1))

        block = ctx.enter_context(nc.Block())

        def high(a):
            return a.bitcast(bf16)[:, 1::2]

        def kv_bank(step, u):
            return ps_kv[:, (KV_POS[u] + NKV * step.par) % 2, :]

        def c_high(par, k, n0, n):
            return cbuf[par][:, k, :].bitcast(bf16)[:, 2 * n0 + 1:2 * (n0 + n):2]

        def p_high(slot, c0, n):
            return prob[slot][:, :].bitcast(bf16)[:, 2 * c0 + 1:2 * (c0 + n):2]

        @block.sync
        def _(sp):
            sp.dma_start(x_all[:, :].rearrange("p (t d) -> p t d", t=TILES),
                         x.rearrange("(t p) d -> p t d", p=P)).then_inc(ld_x, 16)
            sp.dma_start(wq_sb, wqT.rearrange("(k p) n -> p k n", p=P)).then_inc(ld_wq, 16)
            sp.dma_start(cbuf[0][:, :, :], ctxT[0].rearrange("(k p) n -> p k n", p=P)).then_inc(c_loaded[0], 16)

            def steps(step):
                par = step.par
                now, nxt = step.at(1, 0), step.at(1, 2)
                wait(sp, score_done, step, 2 * NCH, -2 * NCH)
                src = q_dram[bass.ds(now, 1)] if step.i is not None else q_dram[step.u:step.u + 1]
                sp.dma_start(qstack[par][0:96, :, :], src[0]).then_inc(q_loaded, 16)
                for t in range(KT):
                    wait(sp, kv_free, step, NKV, KV_POS[NPIECE * (t + 1) - 1] + 1)
                    for r in range(4):
                        for g, src in enumerate((khigh, klow, khigh)):
                            sp.dma_start(kstack[par][32 * g:32 * g + 32, 4 * t + r, 0:SK],
                                         src[32 * r:32 * r + 32, t, 0:SK]).then_inc(k_stacked[4 * t + r], 16)
                if step.i is not None or step.u + 2 < B:
                    wait(sp, kv_done, step, NKV, NKV)
                    src = ctxT[nxt] if step.i is None else ctxT[bass.ds(nxt, 1)][0]
                    sp.dma_start(cbuf[par][:, :, :], src.rearrange("(k p) n -> p k n", p=P))\
                        .then_inc(c_loaded[par], 16)

            sp.dma_start(kstack[0][96:98, :, :].rearrange("p a n -> p (a n)").bitcast(f32), ones2).then_inc(ld_ones, 16)
            sp.wait_ge(q_ps, 4)
            sp.dma_start(cbuf[1][:, :, :], ctxT[1].rearrange("(k p) n -> p k n", p=P)).then_inc(c_loaded[1], 16)
            sp.wait_ge(qbd_hi_rdy, 2)
            for g, parts in enumerate((qbd_hi, qbd_hi, qbd_lo)):
                if g == 2:
                    sp.wait_ge(qbd_lo_rdy, 2)
                for r in range(4):
                    sp.dma_start(q_dram[:, 32 * g:32 * g + 32, 2 * r:2 * r + 2, :].rearrange("b q t c -> q b (t c)"),
                                 parts[32 * r:32 * r + 32, :, :, :].rearrange("q b t c -> q b (t c)"))\
                        .then_inc(q_sent, 16)
            sp.wait_ge(q_sent, QSENT)
            sp.dma_start(kstack[1][96:98, :, :].rearrange("p a n -> p (a n)").bitcast(f32), ones2).then_inc(ld_ones, 16)
            run_steps(sp, steps, B - 2, B)
            sp.wait_ge(kv_done, NKV * B)
            for k in range(KT):
                sp.dma_start(we_sb[k].rearrange("p (e n) -> p e n", e=E),
                             weT.rearrange("e (k p) n -> k p e n", p=P)[k]).then_inc(ev["out"] if k else ld_e, 16)
            with sp.Fori(0, ROUNDS) as p:
                due = values(sp, p)
                for n in lanes:
                    row = sp.snap(p * (LANES * P) + n * P)
                    sp.wait_ge(ev["y"], due[n])
                    sp.wait_ge(ld_x, 16)
                    sp.dma_start(out[bass.ds(row, P), :], b_y[n]).then_inc(ev["out"], 16)
            sp.wait_ge(ev["out"], 16 * TILES + 16)

        @block.gpsimd
        def _(pool):
            nc.gpsimd.memset(ones_f[:, :], 1.0).then_inc(ones_set, 1)
            nc.gpsimd.memset(half_neg[:, :], -0.5).then_inc(ones_set, 1)
            pool.dma_start(cst[:, :], consts).then_inc(ld_c, 16)
            pool.dma_start(w_f[0][:, :, :], wkT.rearrange("(k p) n -> p k n", p=P)).then_inc(ld_w, 16)
            pool.dma_start(w_f[1][:, :, :], wvT.rearrange("(k p) n -> p k n", p=P)).then_inc(ld_w, 16)
            pool.dma_start(bcol[:, :, :], bqk).then_inc(ld_b, 16)
            pool.wait_ge(ones_set, 2)
            pool.wait_ge(ve0_rdy, 1)
            nc.gpsimd.tensor_tensor(rs0[:, :], ve0[:, :], half_neg[:, :], ALU.pow).then_inc(rs0_rdy, 1)
            pool.dma_start(wo_sb[:, :, :], woT.rearrange("(k p) n -> p k n", p=P)).then_inc(ld_t, 16)
            pool.dma_start(wqkv_sb[:, :, :], wqkv.rearrange("(k p) n -> p k n", p=P)).then_inc(ld_t, 16)
            pool.dma_start(wout_sb[:, :, :], wout.rearrange("(k p) n -> p k n", p=P)).then_inc(ld_t, 16)
            pool.dma_start(wg_sb[:, :, :], wg.rearrange("(k p) n -> p k n", p=P)).then_inc(ld_t, 16)
            pool.dma_start(be_sb[:, :], be).then_inc(ld_t, 16)
            pool.dma_start(brow[:, :, :].rearrange("p a n -> p (a n)"), brows.partition_broadcast(P)).then_inc(ld_t, 16)

            def low_context(par, quarter):
                k, (a, n) = quarter // 2, ((0, 801), (801, 800))[quarter % 2]
                nc.gpsimd.tensor_tensor(clow[par][:, k, a:a + n], cbuf[par][:, k, a:a + n], c_high(par, k, a, n),
                                        ALU.subtract).then_inc(clow_done, 1)

            pool.wait_ge(c_loaded[0], 16)
            for quarter in range(4):
                low_context(0, quarter)
            pool.wait_ge(ld_t, 16 * 6)
            for k in range(KT):
                nc.gpsimd.tensor_tensor(wqkv_low[:, k, :], wqkv_sb[:, k, :], high(wqkv_sb[:, k, :]), ALU.subtract)\
                    .then_inc(wqkv_rdy, 1)

            def steps(step):
                par = step.par
                if step.i is not None or step.u + 1 < B:
                    pool.wait_ge(c_loaded[1 - par], ctx_value(step))
                    wait(pool, kv_done, step, NKV, 0)
                    for quarter in range(4):
                        if LOW_AT[quarter] == 0 or not step.attend:
                            low_context(1 - par, quarter)
                if step.attend:
                    b = 1 - par
                    for nth, k in enumerate(low_chunks(step, 1)[0]):
                        if step.i is not None or step.u + 1 < B:
                            for quarter in range(4):
                                if nth and LOW_AT[quarter] == nth:
                                    low_context(1 - par, quarter)
                        _, n = keys_of(k)
                        slot = P_SLOT[b][k]
                        wait(pool, exp_done, step, 2 * NCH, 2 * k + 2 - 2 * NCH)
                        wait(pool, pv_done, step, NCH, P_PREV[b][k] + 1 - NCH)
                        nc.gpsimd.tensor_tensor(plow[slot][0:n, :], prob[slot][0:n, :], p_high(slot, 0, HP * P)[0:n],
                                                ALU.subtract).then_inc(plow_gps, 1)

            def ctx_value(step):
                loads = 16 * ((step.u + 1) // 2 + 1)
                return loads if step.i is None else step.i * 16 + loads

            run_steps(pool, steps, B - 2, B + 2)

            def inverse_roots(a, due):
                for n in lanes:
                    pool.wait_ge(ev["var" + a], due[n])
                    nc.gpsimd.tensor_tensor(rs[a][n][:, :], ve[a][n][:, :], half_neg[:, 0:1], ALU.pow)\
                        .then_inc(ev["rs" + a], 1)

            def low_rows(a, low, rows, high_rows, due):
                for n in lanes:
                    pool.wait_ge(ev[f"h{a}H"], due[n])
                    nc.gpsimd.tensor_tensor(flat3(low[n]), flat3(rows[n]), flat3(high_rows[n]), ALU.subtract)\
                        .then_inc(ev[f"h{a}L"], 1)

            def emit(p, front, back):
                if front:
                    for dst, src, row, done in ((f_rows, att_all, 0, "att_b"), (f_x, x_all, 1, "xb")):
                        for n in lanes:
                            if back:
                                pool.wait_ge(ev["h1T_ps" if row == 0 else "res"], back[n])
                            col = p * (LANES * D) + n * D
                            rows = src[:, col:col + D] if isinstance(p, int) else src[:, bass.ds(pool.snap(col), D)]
                            nc.gpsimd.tensor_tensor(dst[n], rows, brow[:, row, :], ALU.add).then_inc(ev[done], 1)
                if back:
                    inverse_roots("2", back)
                if front:
                    inverse_roots("1", front)
                if back:
                    low_rows("2", b_low, b_T, b_high, back)
                if front:
                    low_rows("1", f_low, f_T, f_high, front)
                    if back is None:
                        pool.wait_ge(ld_e, 16)
                        pool.wait_ge(ev["out"], 16)
                        for k in range(KT):
                            for a in range(0, E * D, 4 * D):
                                w = we_sb[k][:, a:a + 4 * D]
                                nc.gpsimd.tensor_tensor(we_low[k][:, a:a + 4 * D], w, high(w), ALU.subtract)\
                                    .then_inc(we_rdy, 1)
                    for n in lanes:
                        pool.wait_ge(ev["x1"], front[n])
                        if back:
                            pool.wait_ge(ev["x2"], back[n])
                        nc.gpsimd.tensor_tensor(b_res[n], f_x[n], brow[:, 5, :], ALU.add).then_inc(ev["res"], 1)

            pool.wait_ge(att_done, 2 * B)
            rounds(pool, emit)

        @block.tensor
        def _(pe):
            pe.wait_ge(ld_c, 16)
            for t in range(TILES):
                pe.wait_ge(h0_rdy, t + 1)
                if t >= 2:
                    pe.wait_ge(h0T_rdy, t - 1)
                for k in range(KT):
                    mm = nc.tensor.transpose(ps_front[:, t % 2, k * P:(k + 1) * P],
                                             h0[:, t % 4, k * P:(k + 1) * P], ident)
                mm.then_inc(h0T_ps, 1)
            pe.wait_ge(ld_wq, 16)
            pe.wait_ge(h0T_rdy, TILES)
            for o in range(KT):
                for half in range(2):
                    for k, hT in enumerate(h0T):
                        mm = nc.tensor.matmul(ps_score[:, half, :] if o == 0 else ps_out[:, half, :],
                                              wq_sb[:, k, o * P:(o + 1) * P], hT[:, half * 512:half * 512 + 512],
                                              start=(k == 0), stop=(k == KT - 1))
                    mm.then_inc(q_ps, 1)
            pe.wait_ge(w_rdy, 4)

            def project(step, u):
                par = step.par
                wait(pe, kv_free, step, NKV, KV_POS[u] - 1)
                ps = kv_bank(step, u)
                if u < KUNITS:
                    t, n = divmod(u, NPIECE)
                    n0, nn = piece(n)
                    terms = [(w, c, k) for k in range(KT) for w, c in ((w_hi, 0), (w_hi, 1), (w_lo, 0))]
                    for j, (w, c, k) in enumerate(terms):
                        rhs = clow[par][:, k, n0:n0 + nn] if c else c_high(par, k, n0, nn)
                        mm = nc.tensor.matmul(ps[:, 0:nn], w[0][:, k, t * P:(t + 1) * P], rhs,
                                              start=(j == 0), stop=(j == len(terms) - 1))
                else:
                    c0 = 2 * (u - KUNITS)
                    for a, c in enumerate(range(c0, min(c0 + 2, NCH))):
                        n0, nn = keys_of(c)
                        terms = [(w, hi, k) for k in range(KT) for w, hi in ((w_hi, 1), (w_lo, 1), (w_hi, 0))]
                        for j, (w, hi, k) in enumerate(terms):
                            lhs = c_high(par, k, n0, nn) if hi else clow[par][:, k, n0:n0 + nn]
                            mm = nc.tensor.matmul(ps[0:nn, a * D:(a + 1) * D], lhs, w[1][:, k, :],
                                                  start=(j == 0), stop=(j == len(terms) - 1))
                mm.then_inc(kv_done, 1)

            def max_scores(step, m):
                par = step.par
                ps = ps_front[:, front_pos(m) % 2, :]
                bank_free(step, front_pos(m))
                if m == 0:
                    wait(pe, q_loaded, step, 16, 16)
                for at, hp, n in max_unit(m):
                    n0, nn = piece(n)
                    if n == 0:
                        wait(pe, k_stacked[hp], step, 48, 48)
                    mm = nc.tensor.matmul(ps[:, at:at + nn], qstack[par][0:96, q_at(hp), :],
                                          kstack[par][0:96, hp, n0:n0 + nn], start=True, stop=True)
                mm.then_inc(m_done, 1)

            def bank_free(step, pos, back=0):
                pos, back = (pos - 2, back) if pos >= 2 else (pos - 2 + NM, back + 1)
                if pos in SHIFT_POS:
                    wait(pe, shift_copied, step, 2, SHIFT_POS.index(pos) + 1 - 2 * back)
                else:
                    wait(pe, m_free, step, MUNITS, pos - (pos > SHIFT_POS[0]) + 1 - MUNITS * back)

            def shift_rows(step, half, back):
                wait(pe, shift_ready, step, 2, half + 1 - 2 * back)
                bank_free(step, SHIFT_POS[half], back)
                for j in range(4):
                    mm = nc.tensor.matmul(ps_front[96:98, SHIFT_POS[half] % 2, j * P:(j + 1) * P],
                                          mparts[:, 4 * half + j, :], ident_bf[:, :], start=True, stop=True,
                                          tile_position=(0, 96))
                mm.then_inc(shift_done, 1)

            def score_half(step, h):
                k, e = divmod(h, 2)
                n0, nn = keys_of(k)
                par = 1 - step.par
                wait(pe, exp_done, step, 2 * NCH, S_PREV[h] + 1 - 2 * NCH)
                if k == 0:
                    wait(pe, shift_copied, step, 2, e - 1)
                for j in range(4):
                    hp = 4 * e + j
                    mm = nc.tensor.matmul(ps_score[0:nn, S_BANK[h], j * P:(j + 1) * P],
                                          kstack[par][0:98, hp, n0:n0 + nn], qstack[par][0:98, q_at(hp), :],
                                          start=True, stop=True)
                mm.then_inc(score_done, 1)

            def weigh(step, k, back, half):
                b = (step.par + back) % 2
                n0, nn = keys_of(k)
                slot = P_SLOT[b][k]
                if half == 0:
                    gps, dve = low_chunks(step, back)
                    if k in gps:
                        wait(pe, plow_gps, step, len(GPS_CHUNKS), gps.index(k) + 1 - back * len(GPS_CHUNKS))
                    else:
                        wait(pe, plow_dve, step, len(DVE_CHUNKS), dve.index(k) + 1 - back * len(DVE_CHUNKS))
                    if k == 0:
                        wait(pe, out_copied, step, 1, -back)
                for hp in range(4 * half, 4 * half + 4):
                    o = ps_out[:, half, (hp % 4) * OW:(hp % 4 + 1) * OW]
                    for part in range(2):
                        lhs = plow[slot][0:nn, hp * P:(hp + 1) * P] if part else p_high(slot, hp * P, P)[0:nn]
                        mm = nc.tensor.matmul(o, lhs, vstack[b][0:nn, k, hp, 0:OW],
                                              start=(k == 0 and part == 0 and hp % 4 == 0),
                                              stop=(k == NCH - 1 and part == 1 and hp % 4 == 3),
                                              skip_group_check=True)
                if half == 1:
                    mm.then_inc(pv_done, 1)

            def steps(step):
                def weigh_part(k, half):
                    if k >= 2 and step.attend:
                        weigh(step, k - 2, 1, half)
                    if k < 2 and step.tail:
                        weigh(step, NCH - 2 + k, 2, half)

                for k in range(NCH):
                    ms = list(M_SLOTS[k]) if step.front else []
                    kv = list(KV_SLOTS[k]) if step.front else []

                    if k == 0 and step.front:
                        pe.wait_ge(c_loaded[step.par], step.half(1) * 16)
                        wait(pe, clow_done, step, 4, 4)
                    if k == 0 and step.i is None and step.u == 1:
                        pe.wait_ge(fills_set, 2)
                        pe.wait_ge(ld_ones, 32)
                    if k == SHIFT_SLOT and step.front:
                        shift_rows(step, 0, 0)
                    for what in PE_FIRST if k == 0 else PE_ORDER:
                        if what == "m" and ms:
                            max_scores(step, ms.pop(0))
                        if what == "K" and kv:
                            project(step, kv.pop(0))
                        if what == "R" and step.attend:
                            shift_rows(step, 1, 1)
                        if what in "01" and step.attend:
                            score_half(step, 2 * k + int(what))
                        if what in "wW":
                            weigh_part(k, "wW".index(what))

            run_steps(pe, steps, B, B + 2)

            def transposes(dst, src, need, done, value):
                pe.wait_ge(ev[need], value)
                for j in range(src.shape[1] // P):
                    mm = nc.tensor.transpose(dst[:, j * P:(j + 1) * P], src[:, j * P:(j + 1) * P], ident)
                mm.then_inc(ev[done], 1)

            def product(dst, lhsT, rhs, done):
                for k in range(KT):
                    mm = nc.tensor.matmul(dst, lhsT[:, k, :], rhs(k), start=(k == 0), stop=(k == KT - 1))
                mm.then_inc(done, 1)

            def product3(dst, rows_high, rows_low, w, w_low, done, low_event, value):
                for k in range(KT):
                    for part, rhs in enumerate((high(w(k)), w_low(k))):
                        nc.tensor.matmul(dst, rows_high[:, k, :], rhs, start=(k == 0 and part == 0), stop=False)
                pe.wait_ge(ev[low_event], value)
                for k in range(KT):
                    mm = nc.tensor.matmul(dst, rows_low[:, k, :], high(w(k)), start=False, stop=(k == KT - 1))
                mm.then_inc(done, 1)

            def experts(n, pair, value):
                if pair == 0:
                    pe.wait_ge(ev["h2H"], value)
                cols = slice(2 * pair * D, 2 * (pair + 1) * D)
                product3(b_bank[n][pair % 2], b_high[n], b_low[n], lambda k: we_sb[k][:, cols],
                         lambda k: we_low[k][:, cols], e_ps[pair], "h2L", value)

            pe.wait_ge(ld_t, 16 * 6)
            pe.wait_ge(ld_e, 16)
            pe.wait_ge(ev["out"], 16)
            pe.wait_ge(wqkv_rdy, KT)
            pe.wait_ge(ones_set, 2)

            def emit(p, front, back):
                for n in lanes if back else ():
                    pe.wait_ge(y_step[n], added(p, -2))
                    transposes(b_bank[n][0], b_rows[n], "att2", "att2T_ps", back[n])
                for n in lanes if front else ():
                    transposes(f_bank[n][0], f_rows[n], "att_b", "attT_ps", front[n])
                for n in lanes if back else ():
                    pe.wait_ge(ev["att2T"], back[n])
                    pe.wait_ge(y_step[n], added(p, 0))
                    product(b_bank[n][1][:, 0:D], b_T[n], lambda k: wout_sb[:, k, :], ev["w_ps"])
                for n in lanes if front else ():
                    pe.wait_ge(ev["attT"], front[n])
                    product(f_bank[n][1][:, 0:D], f_T[n], lambda k: wo_sb[:, k, :], ev["o_ps"])
                for n in lanes if back else ():
                    transposes(b_bank[n][0], b_rows[n], "h2", "h2T_ps", back[n])
                for n in lanes if front else ():
                    transposes(f_bank[n][0], f_rows[n], "h1", "h1T_ps", front[n])
                for n in lanes if back else ():
                    pe.wait_ge(ev["h2T"], back[n])
                    product(b_bank[n][1][:, 0:E], b_T[n], lambda k: wg_sb[:, k, :], ev["lg_ps"])
                for n in lanes if front else ():
                    pe.wait_ge(ev["h1H"], front[n])
                    for dst, cols, done in ((f_bank[n][0], slice(0, 2 * D), "qk_ps"),
                                            (f_bank[n][1][:, 0:D], slice(2 * D, 3 * D), "v_ps")):
                        product3(dst, f_high[n], f_low[n], lambda k: wqkv_sb[:, k, cols],
                                 lambda k: wqkv_low[:, k, cols], ev[done], "h1L", front[n])
                for n in lanes if back else ():
                    pe.wait_ge(ev["mask"], back[n])
                    pe.wait_ge(ev["before"], back[n])
                    nc.tensor.matmul(locations(n), tri, mask[n][:, :], start=True, stop=False)
                    nc.tensor.matmul(locations(n), ones_f[:, :], before[n][:, :], start=False, stop=True)\
                        .then_inc(ev["loc_ps"], 1)
                for n in lanes if front else ():
                    transposes(f_bank[n][0], rot[n], "rot", "rT_ps", front[n])
                if back:
                    pe.wait_ge(we_rdy, 2 * KT)
                for n in lanes if back else ():
                    experts(n, 0, back[n])
                for n in lanes if back else ():
                    pe.wait_ge(ev["wgt"], back[n])
                    nc.tensor.transpose(weights_T(n), wgt[n][:, :], ident).then_inc(ev["wT_ps"], 1)
                for n in lanes if back else ():
                    pe.wait_ge(ev["wT"], back[n])
                    nc.tensor.matmul(biases(n), wT[n][:, :], be_sb[:, :], start=True, stop=True).then_inc(ev["b_ps"], 1)
                for n in lanes if front else ():
                    pe.wait_ge(ev["kbd"], front[n])
                    pe.wait_ge(ev["v"], front[n])
                    for g in range(2):
                        for b in range(2):
                            mm = nc.tensor.matmul(f_bank[n][g][64 * b:64 * b + 64, :], qkT[n][:, g, 64 * b:64 * b + 64],
                                                  kbd[n][:, g, b, :], start=True, stop=True)
                        mm.then_inc(ev[f"s_ps{g}"], 1)
                for n in lanes if back else ():
                    pe.wait_ge(ev["y0"], back[n])
                    experts(n, 1, back[n])
                for n in lanes if front else ():
                    for g in range(2):
                        transposes(f_bank[n][g], sc[n][:, g, :], "exp", f"pT_ps{g}", front[n])
                for n in lanes if back else ():
                    pe.wait_ge(y_step[n], added(p, 2))
                    experts(n, 2, back[n])
                for n in lanes if front else ():
                    pe.wait_ge(ev["pT"], front[n])
                    for hp in range(HP):
                        for b in range(2):
                            mm = nc.tensor.matmul(f_bank[n][0][64 * b:64 * b + 64, hp * 32:(hp + 1) * 32],
                                                  pT[n][:, hp, 64 * b:64 * b + 64],
                                                  vbd[n][:, b, hp, :, :].rearrange("p j d -> p (j d)"),
                                                  start=True, stop=True)
                    mm.then_inc(ev["pv_ps"], 1)
                for n in lanes if back else ():
                    pe.wait_ge(y_step[n], added(p, 4))
                    experts(n, 3, back[n])

            rounds(pe, emit)

        @block.scalar
        def _(act):
            for t in range(TILES):
                act.wait_ge(h0T_ps, t + 1)
                for k, hT in enumerate(h0T):
                    cp = nc.scalar.copy(hT[:, t * P:(t + 1) * P], ps_front[:, t % 2, k * P:(k + 1) * P])
                cp.then_inc(h0T_rdy, 1)

            act.wait_ge(qhi_rdy, 1)
            for o in range(KT):
                for j in range(2):
                    cp = nc.scalar.activation(qbd_hi[:, :, o, j * SQ:(j + 1) * SQ],
                                              qhi[o][:, :].rearrange("p (b q) -> p b q", b=B), ACT.Copy,
                                              scale=jmask[:, j:j + 1])
                cp.then_inc(qbd_hi_rdy, 1)

            def high_part(step, u):
                par = step.par
                wait(act, kv_done, step, NKV, KV_POS[u] + 1)
                if u < KUNITS:
                    t, n = divmod(u, NPIECE)
                    n0, nn = piece(n)
                    if n == 0:
                        for r in range(4):
                            wait(act, k_stacked[4 * t + r], step, 48, 0)
                    nc.scalar.activation(khigh[:, t, n0:n0 + nn], kv_bank(step, u)[:, 0:nn], ACT.Identity,
                                         bias=bcol[:, 1, t:t + 1]).then_inc(high_done, 1)
                else:
                    c0 = 2 * (u - KUNITS)
                    nch = min(2, NCH - c0)
                    rows = P if c0 + nch < NCH else LAST
                    if u == KUNITS:
                        wait(act, pv_done, step, NCH, -NCH)
                    nc.scalar.copy(vstack[par][0:rows, c0:c0 + nch, :, 0:32],
                                   kv_bank(step, u)[0:rows, 0:nch * D].rearrange("p (c h d) -> p c h d", c=nch, h=HP))\
                        .then_inc(high_done, 1)

            def exponentials(step, h):
                k, e = divmod(h, 2)
                b = 1 - step.par
                _, nn = keys_of(k)
                slot = P_SLOT[b][k]
                wait(act, score_done, step, 2 * NCH, h + 1 - 2 * NCH)
                if e == 0:
                    wait(act, pv_done, step, NCH, P_PREV[b][k] + 1 - NCH)
                nc.scalar.activation(prob[slot][0:nn, e * 512:e * 512 + 512], ps_score[0:nn, S_BANK[h], :], ACT.Exp)\
                    .then_inc(exp_done, 1)

            def copy_shift(step, half, back):
                wait(act, shift_done, step, 2, half + 1 - 2 * back)
                nc.scalar.copy(qstack[(step.par + back) % 2][96:98, half::2, :],
                               ps_front[96:98, SHIFT_POS[half] % 2, :].rearrange("p (h c) -> p h c", h=4))\
                    .then_inc(shift_copied, 1)

            def steps(step):
                for k in range(NCH):
                    kv = list(KV_SLOTS[k]) if step.front else []
                    if k == SHIFT_SLOT and step.front:
                        copy_shift(step, 0, 0)
                    if k == 2 and step.tail:
                        wait(act, pv_done, step, NCH, -NCH)
                        nc.scalar.copy(osb2[:, :, :], ps_out[:, :, 0:4 * OW]).then_inc(out_copied, 1)
                    for what in ACT_FIRST if k == 0 else ACT_ORDER:
                        if what == "K" and kv:
                            high_part(step, kv.pop(0))
                        if what == "R" and step.attend:
                            copy_shift(step, 1, 1)
                        if what in "01" and step.attend:
                            exponentials(step, 2 * k + int(what))

            run_steps(act, steps, B, B + 2)

            def evacuate(dst, src, need, done, value):
                act.wait_ge(ev[need], value)
                nc.scalar.copy(dst, src).then_inc(ev[done], 1)

            def transposed(rows, src, name, due, high_rows=None):
                for n in lanes:
                    evacuate(flat3(rows[n]), src[n][:, 0:D], name + "T_ps", name + "T", due[n])
                    if high_rows:
                        nc.scalar.copy(flat3(high_rows[n]), src[n][:, 0:D]).then_inc(ev[name + "H"], 1)

            def emit(p, front, back):
                if back:
                    transposed(b_T, [a[0] for a in b_bank], "att2", back)
                if front:
                    transposed(f_T, [a[0] for a in f_bank], "att", front)
                if back:
                    transposed(b_T, [a[0] for a in b_bank], "h2", back, b_high)
                if front:
                    transposed(f_T, [a[0] for a in f_bank], "h1", front, f_high)
                for n in lanes if back else ():
                    act.wait_ge(ev["lneg"], back[n])
                    nc.scalar.activation(ex[n][:, :], lg[n][:, :], ACT.Exp, bias=lneg[n][:, :],
                                         accum_out=lsum[n][:, :])\
                        .then_inc(ev["ex"], 1)
                for n in lanes if front else ():
                    evacuate(flat3(qkT[n]), f_bank[n][0], "rT_ps", "rT", front[n])
                for n in lanes if back else ():
                    evacuate(wT[n][:, :], weights_T(n), "wT_ps", "wT", back[n])
                for n in lanes if front else ():
                    for g in range(2):
                        act.wait_ge(ev[f"sub{g}"], front[n])
                        e = nc.scalar.activation(sc[n][:, g, :], sc[n][:, g, :], ACT.Exp)
                    e.then_inc(ev["exp"], 1)
                for n in lanes if front else ():
                    for g in range(2):
                        act.wait_ge(ev[f"pT_ps{g}"], front[n])
                        cp = nc.scalar.copy(flat3(pT[n])[:, g * 512:(g + 1) * 512], f_bank[n][g])
                    cp.then_inc(ev["pT"], 1)

            rounds(act, emit)

        @block.vector
        def _(dve):
            count = [0]

            def link(ins):
                count[0] += 1
                ins.then_inc(chain0, 1)
                dve.wait_ge(chain0, count[0])

            for p in range(2):
                nc.vector.memset(vstack[p][:, :, :, 64:66], 1.0).then_inc(fills_set, 1)
            dve.wait_ge(ld_x, 16)
            for t in range(TILES):
                st = nc.vector.bn_stats(st0[:, t, :], x_all[:, t * D:(t + 1) * D])
            link(st)
            for t in range(TILES):
                ag = nc.vector.bn_aggr(mv0[:, t, :], st0[:, t, :])
            link(ag)
            nc.vector.tensor_scalar_add(ve0[:, :], mv0[:, :, 1], EPS).then_inc(ve0_rdy, 1)
            dve.wait_ge(ld_b, 16)
            nc.vector.tensor_scalar_mul(bq4[:, :], bcol[:, 0, :], DH ** -0.5)
            dve.wait_ge(ld_c, 16)
            nc.vector.tensor_copy(ident_bf[:, :], ident)
            dve.wait_ge(rs0_rdy, 1)
            for t in range(TILES):
                if t >= 4:
                    dve.wait_ge(h0T_ps, t - 3)
                nc.vector.tensor_scalar(h0[:, t % 4, :], x_all[:, t * D:(t + 1) * D], mv0[:, t, 0:1], rs0[:, t:t + 1],
                                        ALU.subtract, ALU.mult).then_inc(h0_rdy, 1)
            dve.wait_ge(ld_w, 32)
            for n in range(2):
                nc.vector.tensor_copy(w_hi[n][:, :, :], w_f[n][:, :, :]).then_inc(w_rdy, 1)
            dve.wait_ge(w_rdy, 2)
            for n in range(2):
                nc.vector.tensor_tensor(w_lo[n][:, :, :], w_f[n][:, :, :], w_hi[n][:, :, :], ALU.subtract)\
                    .then_inc(w_rdy, 1)
            for o in range(KT):
                for half in range(2):
                    dve.wait_ge(q_ps, 2 * o + half + 1)
                    last = nc.vector.tensor_scalar(
                        qT[o][:, half * 512:half * 512 + 512], ps_score[:, half, :] if o == 0 else ps_out[:, half, :],
                        DH ** -0.5, bq4[:, o:o + 1], ALU.mult, ALU.add)
            link(last)
            for o in range(KT):
                last = nc.vector.tensor_copy(qhi[o][:, :], qT[o][:, :])
            last.then_inc(qhi_rdy, 1)
            dve.wait_ge(qhi_rdy, 1)
            for o in range(KT):
                last = nc.vector.tensor_tensor(qlo[o][:, :], qT[o][:, :], qhi[o][:, :], ALU.subtract)
            link(last)
            for o in range(KT):
                for j in range(2):
                    last = nc.vector.tensor_scalar(qbd_lo[:, :, o, j * SQ:(j + 1) * SQ],
                                                   qlo[o][:, :].rearrange("p (b q) -> p b q", b=B),
                                                   jmask[:, j:j + 1], None, ALU.mult)
                last.then_inc(qbd_lo_rdy, 1)
            nc.vector.memset(before[0][:, :], 0.0).then_inc(ev["before"], 1)

            def low_prob(step, k):
                b = 1 - step.par
                _, nn = keys_of(k)
                slot = P_SLOT[b][k]
                wait(dve, exp_done, step, 2 * NCH, 2 * k + 2 - 2 * NCH)
                wait(dve, pv_done, step, NCH, P_PREV[b][k] + 1 - NCH)
                nc.vector.tensor_tensor(plow[slot][0:nn, :], prob[slot][0:nn, :], p_high(slot, 0, HP * P)[0:nn],
                                        ALU.subtract).then_inc(plow_dve, 1)

            def low_part(step, u):
                par = step.par
                wait(dve, high_done, step, NKV, KV_POS[u] + 1)
                if u < KUNITS:
                    t, n = divmod(u, NPIECE)
                    n0, nn = piece(n)
                    if n == 0:
                        for r in range(4):
                            wait(dve, k_stacked[4 * t + r], step, 48, 0)
                    nc.vector.scalar_tensor_tensor(klow[:, t, n0:n0 + nn], kv_bank(step, u)[:, 0:nn], bcol[:, 1, t:t + 1],
                                                   khigh[:, t, n0:n0 + nn], ALU.add, ALU.subtract).then_inc(kv_free, 1)
                else:
                    c0 = 2 * (u - KUNITS)
                    nch = min(2, NCH - c0)
                    rows = P if c0 + nch < NCH else LAST
                    v = vstack[par][0:rows, c0:c0 + nch, :, :]
                    nc.vector.tensor_tensor(v[:, :, :, 32:64],
                                            kv_bank(step, u)[0:rows, 0:nch * D].rearrange("p (c h d) -> p c h d", c=nch, h=HP),
                                            v[:, :, :, 0:32], ALU.subtract).then_inc(kv_free, 1)

            def maximum(step, m):
                wait(dve, m_done, step, MUNITS, m + 1)
                ps = ps_front[:, front_pos(m) % 2, :]
                unit = max_unit(m)
                _, hp, n = unit[0]
                _, nn = piece(n)
                nc.vector.reduce_max(maxes[:, hp:hp + len(unit), n],
                                     ps[:, 0:len(unit) * nn].rearrange("p (h k) -> p h k", k=nn), AX.X).then_inc(m_free, 1)
                if m % (MUNITS // 2) == MUNITS // 2 - 1:
                    shift(step, m // (MUNITS // 2))

            def shift(step, half):
                hps = slice(4 * half, 4 * half + 4)
                wait(dve, m_free, step, MUNITS, (half + 1) * (MUNITS // 2))
                if half == 0:
                    wait(dve, shift_done, step, 2, 0)
                nc.vector.tensor_reduce(negmax[:, hps], maxes[:, hps, :], AX.X, ALU.max, negate=True).then_inc(max_done, 1)
                wait(dve, max_done, step, 4, 2 * half + 1)
                nc.vector.tensor_copy(mparts[:, hps, 0], negmax[:, hps]).then_inc(max_done, 1)
                wait(dve, max_done, step, 4, 2 * half + 2)
                nc.vector.tensor_tensor(mparts[:, hps, 1], negmax[:, hps], mparts[:, hps, 0], ALU.subtract)\
                    .then_inc(shift_ready, 1)

            def attended(step):
                wait(dve, out_copied, step, 1, -1)
                nc.vector.reciprocal(orec[:, :], osb[:, :, 64])
                nc.vector.tensor_tensor(osum[:, :, :], osb[:, :, 0:32], osb[:, :, 32:64], ALU.add).then_inc(out_summed, 1)
                wait(dve, out_summed, step, 1, -1)
                col = step.half(-1) * D
                rows = slice(64 * step.par, 64 * step.par + 64)
                for j in range(2):
                    half = slice(64 * j, 64 * j + 64)
                    dst = att_all[rows, bass.ds(col, D)] if step.i is not None else att_all[rows, col:col + D]
                    nc.vector.tensor_tensor(dst.rearrange("p (h j d) -> p h j d", h=HP, j=2)[:, :, j, :],
                                            osum[half, :, j * DH:(j + 1) * DH],
                                            orec[half, :].unsqueeze(2).to_broadcast([64, HP, DH]), ALU.mult)\
                        .then_inc(att_done, 1)

            def steps(step):
                for k in range(NCH):
                    ms = list(M_SLOTS[k]) if step.front else []
                    kv = list(KV_SLOTS[k]) if step.front else []
                    for what in DVE_FIRST if k == 0 else DVE_ORDER:
                        if what == "m" and ms:
                            maximum(step, ms.pop(0))
                        if what == "K" and kv:
                            low_part(step, kv.pop(0))
                        if what == "p" and step.attend and k >= 1 and k - 1 in low_chunks(step, 1)[1]:
                            low_prob(step, k - 1)
                        if what == "a" and k == 3 and step.tail:
                            attended(step)
                if step.attend and NCH - 1 in low_chunks(step, 1)[1]:
                    low_prob(step, NCH - 1)

            run_steps(dve, steps, B, B + 2)

            def tt(out_, a, b, op, done, value, need=()):
                for name in need:
                    dve.wait_ge(ev[name], value)
                nc.vector.tensor_tensor(out_, a, b, op).then_inc(ev[done], 1)

            def moments(n, a, x_rows, value):
                dve.wait_ge(ev["x" + a], value)
                nc.vector.bn_stats(stats[a][n][:, :], x_rows).then_inc(ev["stats" + a], 1)
                dve.wait_ge(ev["stats" + a], value)
                nc.vector.tensor_copy(spare[n][:, :], x_rows[:, 0:1])
                nc.vector.bn_aggr(mv[a][n][:, :], stats[a][n][:, :]).then_inc(ev["agg" + a], 1)
                dve.wait_ge(ev["agg" + a], value)
                nc.vector.tensor_scalar_add(ve[a][n][:, :], mv[a][n][:, 1:2], EPS).then_inc(ev["var" + a], 1)

            def normalised(n, a, x_rows, dst, value):
                dve.wait_ge(ev["rs" + a], value)
                nc.vector.tensor_scalar(dst, x_rows, mv[a][n][:, 0:1], rs[a][n][:, :], ALU.subtract, ALU.mult)\
                    .then_inc(ev["h" + a], 1)

            heads = lambda a: a.rearrange("p (h d) -> p h d", d=DH)
            by_key = lambda a: a.rearrange("p (h k) -> p h k", h=8)

            def route(due):
                for n in lanes:
                    dve.wait_ge(ev["lg_ps"], due[n])
                    nc.vector.tensor_copy(lg[n][:, :], b_bank[n][1][:, 0:E]).then_inc(ev["lg"], 1)
                for n in lanes:
                    dve.wait_ge(ev["lg"], due[n])
                    nc.vector.reduce_max(lmax[n][:, :], lg[n][:, :], AX.X).then_inc(ev["lmax"], 1)
                for n in lanes:
                    dve.wait_ge(ev["lmax"], due[n])
                    nc.vector.tensor_scalar_mul(lneg[n][:, :], lmax[n][:, :], -1.0).then_inc(ev["lneg"], 1)
                    nc.vector.scalar_tensor_tensor(eq[n][:, :], lg[n][:, :], lmax[n][:, :], desc, ALU.is_equal, ALU.mult)\
                        .then_inc(ev["ranked"], 1)
                for n in lanes:
                    dve.wait_ge(ev["ranked"], due[n])
                    nc.vector.reduce_max(first[n][:, :], eq[n][:, :], AX.X).then_inc(ev["first"], 1)
                for n in lanes:
                    dve.wait_ge(ev["first"], due[n])
                    nc.vector.tensor_scalar(mask[n][:, :], desc, first[n][:, :], None, ALU.is_equal).then_inc(ev["mask"], 1)

            def count(n, due):
                tt(before[(n + 1) % LANES][:, :], before[n][:, :], mask[n][:, :], ALU.add, "before", due[n],
                   ("mask", "before"))

            def weights(n, due):
                dve.wait_ge(ev["ex"], due)
                nc.vector.reciprocal(gate[n][:, :], lsum[n][:, :]).then_inc(ev["gate"], 1)
                dve.wait_ge(ev["loc_ps"], due)
                nc.vector.scalar_tensor_tensor(keep[n][:, :], locations(n), float(CAP), mask[n][:, :], ALU.is_lt,
                                               ALU.mult).then_inc(ev["keep"], 1)
                dve.wait_ge(ev["keep"], due)
                dve.wait_ge(ev["gate"], due)
                nc.vector.tensor_scalar(wgt[n][:, :], keep[n][:, :], gate[n][:, :], None, ALU.mult).then_inc(ev["wgt"], 1)

            def add_experts(p, pair, due):
                for e in (2 * pair, 2 * pair + 1):
                    for n in lanes:
                        if e % 2 == 0:
                            dve.wait_ge(e_ps[pair], due[n])
                        if e == 0:
                            dve.wait_ge(ev["y0"], due[n])
                        else:
                            dve.wait_ge(y_step[n], added(p, e))
                        nc.vector.scalar_tensor_tensor(b_y[n], b_bank[n][pair % 2][:, (e % 2) * D:(e % 2 + 1) * D],
                                                       wgt[n][:, e:e + 1], b_y[n], ALU.mult, ALU.add)\
                            .then_inc(y_step[n], 1)

            def emit(p, front, back):
                for n in lanes if back else ():
                    tt(b_x[n], b_bank[n][1][:, 0:D], b_res[n], ALU.add, "x2", back[n], ("res", "w_ps"))
                    moments(n, "2", b_x[n], back[n])
                for n in lanes:
                    if front:
                        tt(f_x[n], f_bank[n][1][:, 0:D], f_x[n], ALU.add, "x1", front[n], ("xb", "o_ps"))
                        moments(n, "1", f_x[n], front[n])
                    if back and n == 0:
                        for m in lanes:
                            normalised(m, "2", b_x[m], b_rows[m], back[m])
                for n in lanes if front else ():
                    normalised(n, "1", f_x[n], f_rows[n], front[n])
                if back:
                    route(back)
                    for n in range(LANES - 1):
                        count(n, back)
                for n in lanes if front else ():
                    tt(qk[n], f_bank[n][0], brow[:, 2:4, :].rearrange("p a n -> p (a n)"), ALU.add, "qk", front[n],
                       ("qk_ps",))
                    qh, rh = heads(qk[n]), heads(rot[n])
                    tt(rh[:, :, 0:8], qh[:, :, 0:8], qh[:, :, 1:DH:2], ALU.subtract, "rotA", front[n], ("qk",))
                    tt(rh[:, :, 8:DH], qh[:, :, 8:DH], qh[:, :, 0:DH:2], ALU.add, "rotB", front[n])
                    dve.wait_ge(ev["rotA"], front[n])
                    dve.wait_ge(ev["rotB"], front[n])
                    for a in range(2):
                        part = heads(rot[n][:, a * D:(a + 1) * D])
                        tab = rope[:, a * DH:(a + 1) * DH].unsqueeze(1).to_broadcast([P, HEADS, DH])
                        last = nc.vector.tensor_tensor(part, part, tab, ALU.mult)
                    last.then_inc(ev["rot"], 1)
                for n in lanes if back else ():
                    weights(n, back[n])
                if back:
                    count(LANES - 1, back)
                for n in lanes if front else ():
                    dve.wait_ge(ev["v_ps"], front[n])
                    for b in range(2):
                        rows = slice(64 * b, 64 * b + 64)
                        for j in range(2):
                            vin = f_bank[n][1][rows, 0:D].rearrange("p (h j d) -> p h j d", h=HP, j=2)[:, :, j, :]
                            bin_ = brow[rows, 4, :].rearrange("p (h j d) -> p h j d", h=HP, j=2)[:, :, j, :]
                            last = nc.vector.tensor_tensor(vbd[n][64 * j:64 * j + 64, b, :, j, :], vin, bin_, ALU.add)
                    last.then_inc(ev["v"], 1)
                for n in lanes if front else ():
                    dve.wait_ge(ev["rT"], front[n])
                    for g in range(2):
                        for b in range(2):
                            last = nc.vector.tensor_tensor(
                                by_key(kbd[n][:, g, b, :]),
                                qkT[n][:, 2 + g, 64 * b:64 * b + 64].unsqueeze(1).to_broadcast([P, 8, SQ]),
                                mask8.unsqueeze(2).to_broadcast([P, 8, SQ]), ALU.mult)
                    last.then_inc(ev["kbd"], 1)
                if back:
                    dve.wait_ge(ev["out"], p * (16 * LANES) + (16 - 16 * LANES))
                    for n in lanes:
                        tt(b_y[n], biases(n), b_x[n], ALU.add, "y0", back[n], ("b_ps",))
                    add_experts(p, 0, back)
                for n in lanes if front else ():
                    for g in range(2):
                        dve.wait_ge(ev[f"s_ps{g}"], front[n])
                        nc.vector.reduce_max(smax[n][:, 8 * g:8 * g + 8], by_key(f_bank[n][g]), AX.X)\
                            .then_inc(ev[f"smax{g}"], 1)
                    for g in range(2):
                        tt(by_key(sc[n][:, g, :]), by_key(f_bank[n][g]),
                           smax[n][:, 8 * g:8 * g + 8].unsqueeze(2).to_broadcast([P, 8, SQ]), ALU.subtract, f"sub{g}",
                           front[n], (f"smax{g}",))
                if back:
                    add_experts(p, 1, back)
                for n in lanes if front else ():
                    dve.wait_ge(ev["exp"], front[n])
                    nc.vector.reduce_sum(ssum[n][:, :], sc[n].rearrange("p g (h k) -> p (g h) k", h=8), AX.X)\
                        .then_inc(ev["ssum"], 1)
                    dve.wait_ge(ev["ssum"], front[n])
                    nc.vector.reciprocal(srec[n][:, :], ssum[n][:, :]).then_inc(ev["srec"], 1)
                for n in lanes if front else ():
                    tt(heads(b_rows[n]), heads(f_bank[n][0][:, 0:D]), srec[n][:, :].unsqueeze(2).to_broadcast([P, HEADS, DH]),
                       ALU.mult, "att2", front[n], ("srec", "pv_ps"))
                if back:
                    add_experts(p, 2, back)
                    add_experts(p, 3, back)
                    for n in lanes:
                        dve.wait_ge(y_step[n], added(p, E))
                        nc.vector.tensor_copy(spare[n][:, :], b_y[n][:, 0:1]).then_inc(ev["y"], 1)

            dve.wait_ge(ld_t, 16 * 6)
            dve.wait_ge(att_done, 2 * B)
            for n in lanes:
                nc.vector.memset(vbd[n][:, :, :, :, :], 0.0).then_inc(vbd_zero, 1)
                nc.vector.memset(spare[n][:, :], 0.0).then_inc(y_step[n], E)
            dve.wait_ge(vbd_zero, LANES)
            rounds(dve, emit)


_INS = ["x", "ctxT", "wqT", "wkT", "wvT", "bqk", "woT", "wqkv", "wout", "brows", "wg", "weT", "be", "consts", "ones2"]


def shape_constants():
    c = np.zeros((P, NCONST), np.float32)
    p = np.arange(P)
    c[:, C_ID:C_ID + P] = np.eye(P)
    c[:, C_TRI:C_TRI + P] = p[:, None] < p[None, :]
    c[:, C_MASK:C_MASK + 8] = (p[:, None] // DH) == np.arange(8)[None, :]
    c[:, C_J:C_J + 2] = (p[:, None] // DH % 2) == np.arange(2)[None, :]
    c[:, C_DESC:C_DESC + E] = E - np.arange(E)
    theta = np.float32(10000.0) ** (-np.arange(0, DH, 2, dtype=np.float32) / np.float32(DH))
    freqs = (p % SQ).astype(np.float32)[:, None] * theta[None, :]
    table = np.concatenate([np.sin(freqs), np.cos(freqs)], axis=-1).astype(np.float32)
    c[:, C_ROPE:C_ROPE + DH] = table * np.float32(DH ** -0.5)
    c[:, C_ROPE + DH:] = table
    return c


def kernel(**inputs):
    import numpy as _np
    import concourse.bacc as _bacc
    from concourse import mybir as _mybir
    from concourse.bass_utils import run_bass_kernel_spmd as _run

    a = {k: _np.asarray(v) for k, v in inputs.items()}
    t = lambda v, *axes: _np.ascontiguousarray(_np.transpose(v, axes))
    arrays = {
        "x": a["x"].reshape(B * SQ, D), "ctxT": t(a["ctx_1024"], 0, 2, 1),
        "wqT": t(a["L0_xattn_Wq"], 1, 0),
        "wkT": t(a["L0_xattn_Wk"], 1, 0),
        "wvT": t(a["L0_xattn_Wv"], 1, 0),
        "woT": t(a["L0_xattn_Wo"], 1, 0),
        "wqkv": a["L0_attn_Wqkv"], "wout": a["L0_attn_Wout"],
        "wg": a["L0_ffn_wg"], "weT": t(a["L0_ffn_W"], 0, 2, 1), "be": a["L0_ffn_b"], "consts": shape_constants(),
        "ones2": np.full((2, HP * SKP // 2), ONES2, np.float32),
        "bqk": t(_np.stack([a["L0_xattn_bq"], a["L0_xattn_bk"]]).reshape(2, KT, P), 2, 0, 1),
        "brows": _np.concatenate([a["L0_xattn_bv"], a["L0_xattn_bo"], a["L0_attn_bqkv"], a["L0_attn_bout"]]),
    }
    nc = _bacc.Bacc("TRN2", target_bir_lowering=False, num_devices=1)
    args, ins = [], {}
    for name in _INS:
        v = _np.ascontiguousarray(arrays[name])
        ins[f"in_{name}"] = v
        args.append(nc.dram_tensor(f"in_{name}", v.shape, _mybir.dt.from_np(v.dtype), kind="ExternalInput").ap())
    args.append(nc.dram_tensor("out_0", (B * SQ, D), _mybir.dt.float32, kind="ExternalOutput").ap())
    build(nc, *args)
    r = _run(nc, [ins], core_ids=[0])
    return r.results[0]["out_0"].reshape(B, SQ, D)
```
